# Optimizing a Trainium2 kernel written in Bass

```python
import numpy as np
import jax
import jax.numpy as jnp

def _softmax(x, axis=-1):
    return jax.nn.softmax(x, axis=axis)

def _gelu(x):
    return jax.nn.gelu(x, approximate=True)

def _silu(x):
    return jax.nn.silu(x)

def _sigmoid(x):
    return jax.nn.sigmoid(x)

def _layernorm(x, axis=-1, eps=1e-05):
    m = jnp.mean(x, axis=axis, keepdims=True)
    v = jnp.var(x, axis=axis, keepdims=True)
    return (x - m) / jnp.sqrt(v + eps)

def _scatter_add(tgt, idx, src, axis=0):
    return tgt.at[idx].add(src)

def _segment_sum(src, seg, n):
    return jax.ops.segment_sum(src, seg, n)
kernel_name = 'mk_flamingo_gated_d1_seqx_r8_ed53b6'

def setup_inputs(seed: int=0):
    np.random.seed(seed)
    _w = jnp.asarray

    def _rec_inputs():
        import jax
        import jax.numpy as jnp
        _rk = jax.random.key(seed)
        x = -0.000125 + 0.9999 * jax.random.normal(jax.random.fold_in(_rk, 1), (32, 64, 256), jnp.float32)
        _lenS = 64 - jax.random.randint(jax.random.fold_in(_rk, 7), (32,), 0, max(1, 64 // 4) + 1, jnp.int32)
        _lenS2 = 64 - jax.random.randint(jax.random.fold_in(_rk, 8), (32,), 0, max(1, 64 // 4) + 1, jnp.int32)
        _ctx_2048P = jax.random.normal(jax.random.fold_in(_rk, 11), (32, 16, 256), jnp.float32)
        _ctx_2048c = jax.random.dirichlet(jax.random.fold_in(_rk, 511), 0.3 * jnp.ones((16,), jnp.float32), (32, 64))
        _ctx_2048t = jnp.einsum('bsk,bkd->bsd', _ctx_2048c, _ctx_2048P)
        _ctx_2048t = _ctx_2048t * jax.lax.rsqrt(jnp.mean(jnp.square(_ctx_2048t)) + 1e-12) * 0.953939
        ctx_2048 = -0.000514642 + 1.00011 * (_ctx_2048t + 0.3 * jax.random.normal(jax.random.fold_in(_rk, 611), (32, 64, 256), jnp.float32))
        _validS = jnp.arange(64)[None, :] < _lenS[:, None]
        _validS2 = jnp.arange(64)[None, :] < _lenS2[:, None]
        _causal = jnp.tril(jnp.ones((64, 64), dtype=bool))
        mask_BxS2_bk0 = jnp.logical_not(jnp.broadcast_to(_validS2[:, :], (32, 64)))
        _g = jax.random.normal(jax.random.fold_in(_rk, 9001), (2, 1), jnp.float32)
        _g = jnp.sign(_g) * jnp.maximum(jnp.abs(_g), 1.0) + (_g == 0) * 1.0
        g_xattn = _g[0]
        g_ffn = _g[1]
        return (x, ctx_2048, mask_BxS2_bk0, g_xattn, g_ffn)
    x, ctx_2048, mask_BxS2_bk0, g_xattn, g_ffn = _rec_inputs()

    def _L0_xattn_setup():
        import jax, jax.numpy as jnp
        import numpy as np
        key = jax.random.key(seed)
        k1, k2, k3 = jax.random.split(key, 3)
        B, S, D, M = (8, 256, 256, 128)
        hidden_states = jax.random.normal(k1, (B, S, D), dtype=jnp.float32)
        memory_tokens = jax.random.normal(k2, (B, M, D), dtype=jnp.float32)
        memory_mask = jax.random.randint(k3, (B, M), 0, 2).astype(jnp.bool_)
        return {'hidden_states': hidden_states, 'memory_tokens': memory_tokens, 'memory_mask': memory_mask}
    _L0_xattn_all = _L0_xattn_setup()
    _L0_xattn_in = {k: v for k, v in _L0_xattn_all.items() if k in ()}
    del _L0_xattn_all

    def _L0_ffn_setup():
        import jax, jax.numpy as jnp
        import numpy as np
        H, I, E, TOP_K = (256, 176, 16, 6)
        IS = 352
        NORM_TOPK_PROB = False

        def _silu_and_mul(gate_up):
            d = gate_up.shape[-1] // 2
            g, u = (gate_up[..., :d], gate_up[..., d:])
            return jax.nn.silu(g) * u
        key = jax.random.key(seed)
        ks = jax.random.split(key, 6)
        s = 0.02
        return {'x': jax.random.normal(ks[0], (1, 256, H), jnp.float32), 'gate_w': jax.random.normal(ks[1], (E, H), jnp.float32) * s, 'w1': jax.random.normal(ks[2], (E, 2 * I, H), jnp.float32) * s, 'w2': jax.random.normal(ks[3], (E, H, I), jnp.float32) * s, 'shared_w1': jax.random.normal(ks[4], (2 * IS, H), jnp.float32) * s, 'shared_w2': jax.random.normal(ks[5], (H, IS), jnp.float32) * s}
    _L0_ffn_all = _L0_ffn_setup()
    _L0_ffn_in = {k: v for k, v in _L0_ffn_all.items() if k in ('gate_w', 'w1', 'w2', 'shared_w1', 'shared_w2')}
    del _L0_ffn_all
    return {'x': x, 'ctx_2048': ctx_2048, 'mask_BxS2_bk0': mask_BxS2_bk0, 'g_xattn': g_xattn, 'g_ffn': g_ffn, 'L0_ffn_gate_w': _L0_ffn_in['gate_w'], 'L0_ffn_w1': _L0_ffn_in['w1'], 'L0_ffn_w2': _L0_ffn_in['w2'], 'L0_ffn_shared_w1': _L0_ffn_in['shared_w1'], 'L0_ffn_shared_w2': _L0_ffn_in['shared_w2']}

def reference(x, ctx_2048, mask_BxS2_bk0, g_xattn, g_ffn, L0_ffn_gate_w, L0_ffn_w1, L0_ffn_w2, L0_ffn_shared_w1, L0_ffn_shared_w2):
    import jax
    import jax.numpy as jnp

    def _L0_xattn_ref(hidden_states, memory_tokens, memory_mask):
        import jax, jax.numpy as jnp
        import numpy as np
        B, S, D = hidden_states.shape
        scale = 1.0 / jnp.sqrt(jnp.asarray(D, hidden_states.dtype))
        scores = jnp.einsum('bsd,bmd->bsm', hidden_states, memory_tokens) * scale
        neg_inf = jnp.asarray(-1e+30, scores.dtype)
        scores = jnp.where(memory_mask[:, None, :], scores, neg_inf)
        attn = jax.nn.softmax(scores, axis=-1)
        readout = jnp.einsum('bsm,bmd->bsd', attn, memory_tokens)
        valid_b = jnp.any(memory_mask, axis=-1)
        out = jnp.where(valid_b[:, None, None], readout, jnp.zeros_like(readout))
        return out

    def _L0_ffn_ref(x, gate_w, w1, w2, shared_w1, shared_w2):
        import jax, jax.numpy as jnp
        import numpy as np
        H, I, E, TOP_K = (256, 176, 16, 6)
        IS = 352
        NORM_TOPK_PROB = False

        def _silu_and_mul(gate_up):
            d = gate_up.shape[-1] // 2
            g, u = (gate_up[..., :d], gate_up[..., d:])
            return jax.nn.silu(g) * u
        B, S, Hd = x.shape
        xf = x.reshape(-1, Hd)
        T = xf.shape[0]
        shared_out = _silu_and_mul(xf @ shared_w1.T) @ shared_w2.T
        logits = xf @ gate_w.T
        probs = jax.nn.softmax(logits.astype(jnp.float32), axis=-1)
        routing_weights, selected = jax.lax.top_k(probs, TOP_K)
        if NORM_TOPK_PROB:
            routing_weights = routing_weights / routing_weights.sum(-1, keepdims=True)
        combine = jnp.zeros((T, E), jnp.float32).at[jnp.arange(T)[:, None], selected].add(routing_weights).astype(x.dtype)
        gate_up = jnp.einsum('th,eoh->teo', xf, w1)
        act = _silu_and_mul(gate_up)
        moe_out = jnp.einsum('te,tei,ehi->th', combine, act, w2)
        return (moe_out + shared_out).reshape(B, S, Hd)
    x = x + jnp.tanh(g_xattn[0]) * _L0_xattn_ref(_layernorm(x, axis=-1), ctx_2048, mask_BxS2_bk0)
    x = x + jnp.tanh(g_ffn[0]) * _L0_ffn_ref(_layernorm(x, axis=-1), L0_ffn_gate_w, L0_ffn_w1, L0_ffn_w2, L0_ffn_shared_w1, L0_ffn_shared_w2)
    return x

_drawn_inputs = setup_inputs


def setup_inputs(seed=0):
    import zlib

    import numpy as np

    out = dict(_drawn_inputs(seed))
    spreads = {}
    factors = {'L0_ffn_gate_w': 8.0,
     'L0_ffn_w1': 8.0,
     'L0_ffn_w2': 8.0,
     'L0_ffn_shared_w1': 3.466,
     'L0_ffn_shared_w2': 3.459}
    for name, (base, spread) in spreads.items():
        noise = np.random.default_rng([zlib.crc32(name.encode()), seed]).standard_normal(out[name].shape)
        drawn = base * np.exp(spread * noise) if base else spread * noise
        out[name] = jnp.asarray(drawn.astype(out[name].dtype))
    for name, factor in factors.items():
        out[name] = (out[name] * factor).astype(out[name].dtype)
    return out
```

```python
from contextlib import ExitStack

import concourse.bass as bass
from concourse import mybir

B, S, M, D = 32, 64, 64, 256
P = 128
T = B * S // P
BT = P // S
KC = D // P
E, I, TOPK = 16, 176, 6
SH = 352 // I
NE = E + SH
NP = NE // 2
HID = NE * I
NCH = -(-HID // P)
LAST = HID - (NCH - 1) * P
GC = 4
NG = -(-NCH // GC)
WP = KC * 2 * I
NRAW = 3
EPS = 1e-5
MASKED = -1e30 * D ** 0.5


def chunks(g):
    return range(GC * g, min(GC * g + GC, NCH))


def rows(c):
    return LAST if c == NCH - 1 else P


def last_pair(g):
    return (min(GC * (g + 1) * P, HID) - 1) // (2 * I)


TRANSPOSED = {0: [5 - NG, 6 - NG], 2: [0], 3: [1], 5: [2], 6: [3], 8: [4]}
MULTIPLIED = {0: [4 - NG], 1: [5 - NG, 6 - NG], 3: [0], 4: [1], 6: [2], 7: [3]}

PIECES = []
for _p in range(NP):
    PIECES += [("w1", 2 * _p), ("w1", 2 * _p + 1)]
    for _g in MULTIPLIED.get(_p + 1, []):
        if _g >= 0:
            PIECES += [("w2", c) for c in chunks(_g) if c % 2 == 0]
PIECES += [("w2", c) for c in range(0, NCH, 2) if ("w2", c) not in PIECES]
PLACE = {x: n for n, x in enumerate(PIECES)}


def by_pool(n):
    return n % 3 == 2


def lows(n, pool):
    return sum(by_pool(k) == pool for k in range(n + 1))


def needed_at(p):
    w1 = PLACE[("w1", 2 * p + 1)]
    w2 = [PLACE[("w2", c - c % 2)] for g in MULTIPLIED.get(p, []) if g >= 0 for c in chunks(g)]
    return max([w1] + w2)


FIRST_PIECES = needed_at(1) + 1


def pieces_of(p):
    def upto(q):
        return needed_at(q) + 1 if q < NP else len(PIECES)
    return range(upto(p + 1), upto(min(p + 2, NP)))


def gated_flamingo_block(nc, x, ctx_n, ctx_t, mask, gates, gate_w, w1, w2, ident, sel, out):
    f32, f32r, u8, i32 = mybir.dt.float32, mybir.dt.float32r, mybir.dt.uint8, mybir.dt.int32
    ALU, ACT, AX = mybir.AluOpType, mybir.ActivationFunctionType, mybir.AxisListType

    with ExitStack() as stack:
        def sb(name, shape, dt=f32):
            return stack.enter_context(nc.sbuf_tensor(name, shape, dt))

        def ps(name, shape):
            return stack.enter_context(nc.psum_tensor(name, shape, f32))

        def sem(name):
            return stack.enter_context(nc.semaphore(name))

        W1h, W1l = sb("W1h", [P, NE, KC, 2 * I], f32r), sb("W1l", [P, NE, KC, 2 * I], f32r)
        W2h, W2l = sb("W2h", [P, NCH, D], f32r), sb("W2l", [P, NCH, D], f32r)
        Gh, Gl = sb("Gh", [P, KC, E], f32r), sb("Gl", [P, KC, E], f32r)
        raw = sb("raw", [P, NRAW, WP])
        raw_gate = sb("raw_gate", [P, KC, E])
        identity, selector = sb("identity", [P, P]), sb("selector", [BT, P])
        mask_words, tanh_gates = sb("mask_words", [BT, T, P // 4], i32), sb("tanh_gates", [P, 2])
        mask_in = mask_words[:, :, :].bitcast(u8)
        gates_in = sb("gates_in", [P, 2])
        x_in, ctx_in = sb("x_in", [P, 2, D]), sb("ctx_in", [P, 2, D])
        ctxT_in = sb("ctxT_in", [P, 2, KC, P])
        bias = sb("bias", [BT, P + 2])
        mask_f, eps = sb("mask_f", [BT, P]), sb("eps", [P, 1])
        any_valid = sb("any_valid", [BT, T, 2])
        xn, xnT = sb("xn", [P, D]), sb("xnT", [P, KC, P])
        stats, moments = sb("stats", [P, 2, 6]), sb("moments", [P, 2, 2])
        newton = sb("newton", [P, 2, 8])
        small = sb("small", [P, 8])
        probs, probsT = sb("probs", [P, M * BT]), sb("probsT", [M * BT, P])
        x2, x2n = sb("x2", [P, 2, D]), sb("x2n", [P, D])
        xTh, xTl = sb("xTh", [P, 2, KC, P], f32r), sb("xTl", [P, 2, KC, P], f32r)
        route = sb("route", [P, 3, E])
        top8 = sb("top8", [P, 8])
        combine = sb("combine", [P, 2, NE])
        gated = sb("gated", [P, 2, 2, I])
        hidden = sb("hidden", [P, HID])
        hTh, hTl = sb("hTh", [P, 2, GC, P], f32r), sb("hTl", [P, 2, GC, P], f32r)
        y = sb("y", [P, 2, D])

        up_ps = ps("up_ps", [P, 2, 2, 512])
        hT_ps = ps("hT_ps", [P, 2, GC, P])
        out_ps = ps("out_ps", [P, 512])
        front_ps = ps("front_ps", [P, 512])
        xT_ps = front_ps[:, 0:D].rearrange("p (c n) -> p c n", c=KC)
        score_ps = front_ps[:, D:D + P]
        probsT_ps = front_ps[:, 0:P]
        read_ps = front_ps[:, P:P + D]
        valid_ps = front_ps[:, 384:386]
        logit_ps = front_ps[:, 400:400 + E]

        consts_in = sem("consts_in")
        tile_in = [sem("tile_in_even"), sem("tile_in_odd")]
        raw_in = [sem(f"raw_in_{k}") for k in range(NRAW)]
        y_out = [sem("y_out_even"), sem("y_out_odd")]
        high_made, low_by_vector, low_by_pool = sem("high_made"), sem("low_by_vector"), sem("low_by_pool")
        gate_parts = sem("gate_parts")
        tanh_made = sem("tanh_made")
        any_valid_made, bias_made = sem("any_valid_made"), sem("bias_made")
        moments_made = sem("moments_made")
        rstd_made = sem("rstd_made")
        normed = sem("normed")
        normedT_ps, xnT_made = sem("normedT_ps"), sem("xnT_made")
        scored, max_made, exp_made = sem("scored"), sem("max_made"), sem("exp_made")
        probsT_done, probsT_made, readout_done = sem("probsT_done"), sem("probsT_made"), sem("readout_done")
        x2_made = sem("x2_made")
        xTh_made, xTl_made = sem("xTh_made"), sem("xTl_made")
        logits_done, logit_max, route_exp, combine_made = (
            sem("logits_done"), sem("logit_max"), sem("route_exp"), sem("combine_made"))
        vector_step, pool_step = sem("vector_step"), sem("pool_step")
        up_done, tanh_done, hidden_made = sem("up_done"), sem("tanh_done"), sem("hidden_made")
        gated_made = sem("gated_made")
        hT_done, hTh_made, hTl_made, down_done = (
            sem("hT_done"), sem("hTh_made"), sem("hTl_made"), sem("down_done"))
        y_made = sem("y_made")

        block = stack.enter_context(nc.Block())

        def tiles(eng, step, ending):
            step(0, 0, 0, first=True)
            with eng.Fori(0, (T - 2) // 2) as i:
                step(i * 2 + 1, 1, i)
                step(i * 2 + 2, 0, i + 1)
            step(T - 1, 1, (T - 2) // 2, front=False)
            ending()

        @block.sync
        def _(sp):
            def load_tile(t, par, wait=True):
                if wait:
                    sp.wait_ge(x2_made, t - 1)
                sp.dma_start(x_in[:, par, :], x[bass.ds(t * P, P), :]).then_inc(tile_in[par], 16)
                sp.dma_start(ctxT_in[:, par, :, :], ctx_t[:, bass.ds(t, 1), :, :].rearrange("p t c m -> p (t c) m")
                             ).then_inc(tile_in[par], 16)
                sp.dma_start(ctx_in[:, par, :], ctx_n[bass.ds(t * P, P), :]).then_inc(tile_in[par], 16)

            def load_piece(n):
                kind, k = PIECES[n]
                if n >= NRAW:
                    m = n - NRAW
                    if by_pool(m):
                        sp.wait_ge(low_by_pool, lows(m, True))
                    else:
                        sp.wait_ge(low_by_vector, lows(m, False))
                if kind == "w1":
                    src, cols = w1[k, :, :], WP
                else:
                    c = min(2, NCH - k)
                    src, cols = w2[:, k * D:(k + c) * D], c * D
                sp.dma_start(raw[:, n % NRAW, 0:cols], src).then_inc(raw_in[n % NRAW], 16)

            for par in range(2):
                sp.sem_inc(y_out[par], 16)
            load_tile(0, 0, wait=False)
            for dst, src in ((mask_words[:, :, :], mask), (identity[:, :], ident), (selector[:, :], sel),
                             (gates_in[:, :], gates), (raw_gate[:, :, :], gate_w)):
                sp.dma_start(dst, src).then_inc(consts_in, 16)
            for n in range(4):
                load_piece(n)
            load_tile(1, 1, wait=False)
            for n in range(4, len(PIECES)):
                load_piece(n)

            def store(t, par):
                sp.wait_ge(y_made, t + 1)
                sp.dma_start(out[bass.ds(t * P, P), :], y[:, par, :]).then_inc(y_out[par], 16)

            with sp.Fori(0, (T - 2) // 2) as i:
                load_tile(i * 2 + 2, 0)
                store(i * 2, 0)
                load_tile(i * 2 + 3, 1)
                store(i * 2 + 1, 1)
            store(T - 2, 0)
            store(T - 1, 1)
            for par in range(2):
                sp.wait_ge(y_out[par], 16 * (T // 2) + 16)

        @block.tensor
        def _(pe):
            def split_product(dst, lh, ll, rh, rl, start, stop):
                nc.tensor.matmul(dst, lh, rh, start=start, stop=False)
                nc.tensor.matmul(dst, lh, rl, start=False, stop=False)
                return nc.tensor.matmul(dst, ll, rh, start=False, stop=stop)

            def transposes(src, sems, value):
                for c in range(KC):
                    last = nc.tensor.transpose(xT_ps[:, c, :], src[:, c * P:(c + 1) * P], identity[:, :])
                last.then_inc(normedT_ps, 1)

            def front_normed(u, par, first=False):
                if first:
                    pe.wait_ge(consts_in, 16 * 5)
                else:
                    pe.wait_ge(route_exp, u)
                pe.wait_ge(normed, 2 * u + 1)
                transposes(xn, normedT_ps, 2 * u + 1)

            def front_scores(u, par, first=False):
                pe.wait_ge(bias_made, u + 1)
                pe.wait_ge(xnT_made, u + 1)
                nc.tensor.matmul(valid_ps, selector[:, :], bias[:, P:P + 2], start=True, stop=True)
                nc.tensor.matmul(score_ps, selector[:, :], bias[:, 0:P], start=True, stop=False)
                for c in range(KC):
                    last = nc.tensor.matmul(score_ps, xnT[:, c, :], ctxT_in[:, par, c, :],
                                            start=False, stop=c == KC - 1)
                last.then_inc(scored, 1)

            def front_probs(u, par, first=False):
                pe.wait_ge(exp_made, u + 1)
                nc.tensor.transpose(probsT_ps, probs[:, :], identity[:, :]).then_inc(probsT_done, 1)

            def front_readout(u, par, first=False):
                pe.wait_ge(probsT_made, u + 1)
                nc.tensor.matmul(read_ps, probsT[:, :], ctx_in[:, par, :], start=True, stop=True
                                 ).then_inc(readout_done, 1)

            def front_x2(u, par, first=False):
                pe.wait_ge(normed, 2 * u + 2)
                transposes(x2n, normedT_ps, 2 * u + 2)

            def front_logits(u, par, first=False):
                pe.wait_ge(xTl_made, u + 1)
                if first:
                    pe.wait_ge(gate_parts, 2)
                parts = [(a, b) for a in (xTh, xTl) for b in (Gh, Gl)]
                for n, (a, b) in enumerate(parts):
                    for c in range(KC):
                        last = nc.tensor.matmul(logit_ps, a[:, par, c, :], b[:, c, :],
                                                start=n == 0 and c == 0, stop=n == 3 and c == KC - 1)
                last.then_inc(logits_done, 1)

            FRONT = {2: front_normed, 3: front_scores, 4: front_probs, 5: front_readout,
                     7: front_x2, 8: front_logits}

            def up(t, par, p, first):
                ring = (par + p) % 2
                if not (first and p < 2):
                    pe.wait_ge(hidden_made, t * NP + p - 1)
                for e in range(2):
                    blk = 2 * p + e
                    for c in range(KC):
                        last = split_product(up_ps[:, ring, e, 0:2 * I], xTh[:, par, c, :], xTl[:, par, c, :],
                                             W1h[:, blk, c, :], W1l[:, blk, c, :], c == 0, c == KC - 1)
                last.then_inc(up_done, 1)

            def transpose_group(t, par, g):
                ring = (par + g) % 2
                pe.wait_ge(hidden_made, t * NP + last_pair(g) + 1)
                if not (isinstance(t, int) and t * NG + g < 2):
                    pe.wait_ge(hTl_made, t * NG + g - 1)
                for n, c in enumerate(chunks(g)):
                    last = nc.tensor.transpose(hT_ps[0:rows(c), ring, n, :], hidden[:, c * P:c * P + rows(c)],
                                               identity[:, :])
                last.then_inc(hT_done, 1)

            def down(t, par, g):
                ring = (par + g) % 2
                if g == 0 and not (isinstance(t, int) and t == 0):
                    pe.wait_ge(y_made, t)
                pe.wait_ge(hTl_made, t * NG + g + 1)
                for n, c in enumerate(chunks(g)):
                    r = rows(c)
                    last = split_product(out_ps[:, 0:D], hTh[0:r, ring, n, :], hTl[0:r, ring, n, :],
                                         W2h[0:r, c, :], W2l[0:r, c, :], c == 0, c == NCH - 1)
                last.then_inc(down_done, 1)

            def step(t, par, h, first=False, front=True):
                for p in range(NP):
                    if first:
                        n = needed_at(p)
                        pe.wait_ge(low_by_vector, lows(n, False))
                        if lows(n, True):
                            pe.wait_ge(low_by_pool, lows(n, True))
                    up(t, par, p, first)
                    for g in TRANSPOSED.get(p, []):
                        if g >= 0:
                            transpose_group(t, par, g)
                        elif not first:
                            transpose_group(t - 1, 1 - par, g + NG)
                    for g in MULTIPLIED.get(p, []):
                        if g >= 0:
                            down(t, par, g)
                        elif not first:
                            down(t - 1, 1 - par, g + NG)
                    if front and p in FRONT:
                        FRONT[p](t + 1, 1 - par)
                if first:
                    pe.wait_ge(low_by_vector, lows(len(PIECES) - 1, False))
                    pe.wait_ge(low_by_pool, lows(len(PIECES) - 1, True))

            def ending():
                for g in (5, 6):
                    transpose_group(T - 1, 1, g)
                for g in (4, 5, 6):
                    down(T - 1, 1, g)

            for p in sorted(FRONT):
                FRONT[p](0, 0, first=True)

            tiles(pe, step, ending)

        @block.scalar
        def _(act):
            def front_xnT(u, par):
                act.wait_ge(normedT_ps, 2 * u + 1)
                nc.scalar.copy(xnT[:, :, :], xT_ps).then_inc(xnT_made, 1)

            def front_exp(u, par):
                act.wait_ge(max_made, u + 1)
                nc.scalar.activation(probs[:, :], score_ps, ACT.Exp, bias=small[:, 1:2], scale=D ** -0.5,
                                     accum_out=small[:, 2:3]).then_inc(exp_made, 1)

            def front_probsT(u, par):
                act.wait_ge(probsT_done, u + 1)
                nc.scalar.copy(probsT[:, :], probsT_ps).then_inc(probsT_made, 1)

            def front_xTh(u, par):
                act.wait_ge(normedT_ps, 2 * u + 2)
                nc.scalar.copy(xTh[:, par, :, :], xT_ps).then_inc(xTh_made, 1)

            def front_route(u, par):
                act.wait_ge(logit_max, u + 1)
                nc.scalar.activation(route[:, 0, :], logit_ps, ACT.Exp, bias=small[:, 5:6],
                                     accum_out=small[:, 6:7]).then_inc(route_exp, 1)

            FRONT = {2: front_xnT, 3: front_exp, 4: front_probsT, 7: front_xTh, 8: front_route}

            def high(n):
                kind, k = PIECES[n]
                act.wait_ge(raw_in[n % NRAW], 16 * (n // NRAW + 1))
                if kind == "w1":
                    nc.scalar.copy(W1h[:, k, :, :], raw[:, n % NRAW, 0:WP].rearrange("p (c n) -> p c n", c=KC)
                                   ).then_inc(high_made, 1)
                else:
                    c = min(2, NCH - k)
                    nc.scalar.copy(W2h[:, k:k + c, :], raw[:, n % NRAW, 0:c * D].rearrange("p (c n) -> p c n", c=c)
                                   ).then_inc(high_made, 1)

            def hidden_high(t, par, g):
                ring, n = (par + g) % 2, len(chunks(g))
                r = rows(chunks(g)[-1]) if n == 1 else P
                act.wait_ge(hT_done, t * NG + g + 1)
                if not (isinstance(t, int) and t * NG + g < 2):
                    act.wait_ge(down_done, t * NG + g - 1)
                nc.scalar.copy(hTh[0:r, ring, 0:n, :], hT_ps[0:r, ring, 0:n, :]).then_inc(hTh_made, 1)

            def step(t, par, h, first=False, front=True):
                for p in range(NP):
                    act.wait_ge(up_done, t * NP + p + 1)
                    ring = (par + p) % 2
                    nc.scalar.activation(gated[:, ring, :, :], up_ps[:, ring, :, 0:I], ACT.Tanh, scale=0.5
                                         ).then_inc(tanh_done, 1)
                    for g in TRANSPOSED.get(p, []):
                        if g >= 0:
                            hidden_high(t, par, g)
                        elif not first:
                            hidden_high(t - 1, 1 - par, g + NG)
                    if front and p in FRONT:
                        FRONT[p](t + 1, 1 - par)
                    if first:
                        for n in pieces_of(p):
                            high(n)

            act.wait_ge(consts_in, 16 * 5)
            nc.scalar.activation(tanh_gates[:, :], gates_in[:, :], ACT.Tanh).then_inc(tanh_made, 1)
            nc.scalar.copy(Gh[:, :, :], raw_gate[:, :, :]).then_inc(gate_parts, 1)
            for k, p in enumerate(sorted(FRONT)):
                FRONT[p](0, 0)
                if k < FIRST_PIECES:
                    high(k)

            def ending():
                for g in (5, 6):
                    hidden_high(T - 1, 1, g)

            tiles(act, step, ending)

        @block.vector
        def _(dve):
            def chained(ins, value):
                ins.then_inc(vector_step, 1)
                dve.wait_ge(vector_step, value)

            def front_moments(u, par, h, first=False):
                dve.wait_ge(tile_in[par], h * 48 + 48)
                chained(nc.vector.bn_stats(stats[:, 0, :], x_in[:, par, :]), 1)
                nc.vector.bn_aggr(moments[:, 0, :], stats[:, 0, :]).then_inc(moments_made, 1)
                dve.sem_clear(vector_step)

            def front_norm(u, par, h, first=False):
                dve.wait_ge(rstd_made, 2 * u + 1)
                nc.vector.tensor_scalar(xn[:, :], x_in[:, par, :], moments[:, 0, 0:1], newton[:, 0, 7:8],
                                        ALU.subtract, ALU.mult).then_inc(normed, 1)

            def front_max(u, par, h, first=False):
                if first:
                    dve.wait_ge(tanh_made, 1)
                dve.wait_ge(scored, u + 1)
                nc.vector.tensor_scalar(small[:, 3:4], valid_ps[:, 0:1], tanh_gates[:, 0:1], None, ALU.mult)
                chained(nc.vector.tensor_reduce(out=small[:, 0:1], in_=score_ps, axis=AX.X, op=ALU.max),
                        1)
                nc.vector.tensor_scalar(small[:, 1:2], small[:, 0:1], -(D ** -0.5), None, ALU.mult
                                        ).then_inc(max_made, 1)
                dve.sem_clear(vector_step)

            def front_attend(u, par, h, first=False):
                dve.wait_ge(exp_made, u + 1)
                chained(nc.vector.reciprocal(small[:, 4:5], small[:, 2:3]), 1)
                chained(nc.vector.tensor_scalar(small[:, 7:8], small[:, 4:5], small[:, 3:4], None, ALU.mult),
                        2)
                dve.sem_clear(vector_step)
                dve.wait_ge(readout_done, u + 1)
                nc.vector.scalar_tensor_tensor(out=x2[:, par, :], in0=read_ps, scalar=small[:, 7:8],
                                               in1=x_in[:, par, :], op0=ALU.mult, op1=ALU.add
                                               ).then_inc(x2_made, 1)
                dve.wait_ge(x2_made, u + 1)
                chained(nc.vector.bn_stats(stats[:, 1, :], x2[:, par, :]), 1)
                nc.vector.bn_aggr(moments[:, 1, :], stats[:, 1, :]).then_inc(moments_made, 1)
                dve.sem_clear(vector_step)

            def front_norm2(u, par, h, first=False):
                dve.wait_ge(rstd_made, 2 * u + 2)
                nc.vector.tensor_scalar(x2n[:, :], x2[:, par, :], moments[:, 1, 0:1], newton[:, 1, 7:8],
                                        ALU.subtract, ALU.mult).then_inc(normed, 1)

            def front_xTl(u, par, h, first=False):
                dve.wait_ge(xTh_made, u + 1)
                nc.vector.tensor_tensor(xTl[:, par, :, :], xT_ps, xTh[:, par, :, :].bitcast(f32), ALU.subtract
                                        ).then_inc(xTl_made, 1)

            def front_router(u, par, h, first=False):
                dve.wait_ge(logits_done, u + 1)
                chained(nc.vector.tensor_reduce(out=small[:, 0:1], in_=logit_ps, axis=AX.X, op=ALU.max),
                        1)
                nc.vector.tensor_scalar(small[:, 5:6], small[:, 0:1], -1.0, None, ALU.mult).then_inc(logit_max, 1)
                dve.sem_clear(vector_step)
                dve.wait_ge(route_exp, u + 1)
                chained(nc.vector.reciprocal(small[:, 4:5], small[:, 6:7]), 1)
                chained(nc.vector.tensor_scalar(route[:, 1, :], route[:, 0, :], small[:, 4:5], 0.5, ALU.mult, ALU.mult),
                        2)
                chained(nc.vector.max(out=top8[:, :], in_=route[:, 1, :]), 3)
                chained(nc.vector.memset(top8[:, TOPK:8], -1.0), 4)
                nc.vector.match_replace(out=route[:, 2, :], in_to_replace=top8[:, :], in_values=route[:, 1, :],
                                        imm_value=0.0).then_inc(combine_made, 1)
                dve.sem_clear(vector_step)
                dve.wait_ge(combine_made, 2 * u + 1)
                nc.vector.tensor_tensor(combine[:, par, 0:E], route[:, 1, :], route[:, 2, :], ALU.subtract
                                        ).then_inc(combine_made, 1)

            FRONT = {0: front_moments, 1: front_norm, 3: front_max, 5: front_attend, 6: front_norm2,
                     7: front_xTl, 8: front_router}

            def low(n):
                kind, k = PIECES[n]
                dve.wait_ge(high_made, n + 1)
                if kind == "w1":
                    nc.vector.tensor_tensor(W1l[:, k, :, :].rearrange("p c n -> p (c n)"), raw[:, n % NRAW, 0:WP],
                                            W1h[:, k, :, :].bitcast(f32).rearrange("p c n -> p (c n)"),
                                            ALU.subtract).then_inc(low_by_vector, 1)
                else:
                    c = min(2, NCH - k)
                    nc.vector.tensor_tensor(W2l[:, k:k + c, :].rearrange("p c n -> p (c n)"), raw[:, n % NRAW, 0:c * D],
                                            W2h[:, k:k + c, :].bitcast(f32).rearrange("p c n -> p (c n)"),
                                            ALU.subtract).then_inc(low_by_vector, 1)

            def hidden_low(t, par, g):
                ring, n = (par + g) % 2, len(chunks(g))
                r = rows(chunks(g)[-1]) if n == 1 else P
                dve.wait_ge(hTh_made, t * NG + g + 1)
                nc.vector.tensor_tensor(hTl[0:r, ring, 0:n, :], hT_ps[0:r, ring, 0:n, :],
                                        hTh[0:r, ring, 0:n, :].bitcast(f32), ALU.subtract).then_inc(hTl_made, 1)

            def result(t, par, h):
                dve.wait_ge(down_done, (t + 1) * NG)
                dve.wait_ge(y_out[par], h * 16 + 16)
                nc.vector.scalar_tensor_tensor(out=y[:, par, :], in0=out_ps[:, 0:D], scalar=tanh_gates[:, 1:2],
                                               in1=x2[:, par, :], op0=ALU.mult, op1=ALU.add).then_inc(y_made, 1)

            def step(t, par, h, first=False, front=True):
                for p in range(NP):
                    ring = (par + p) % 2
                    dve.wait_ge(tanh_done, t * NP + p + 1)
                    nc.vector.scalar_tensor_tensor(out=gated[:, ring, :, :], in0=gated[:, ring, :, :], scalar=1.0,
                                                   in1=up_ps[:, ring, :, 0:I], op0=ALU.add, op1=ALU.mult
                                                   ).then_inc(gated_made, 1)
                    dve.wait_ge(gated_made, t * NP + p + 1)
                    if p == 0:
                        dve.wait_ge(combine_made, 2 * t + 2)
                    for e in range(2):
                        blk = 2 * p + e
                        last = nc.vector.scalar_tensor_tensor(
                            out=hidden[:, blk * I:(blk + 1) * I], in0=gated[:, ring, e, :],
                            scalar=combine[:, par, blk:blk + 1], in1=up_ps[:, ring, e, I:2 * I],
                            op0=ALU.mult, op1=ALU.mult)
                    last.then_inc(hidden_made, 1)
                    for g in TRANSPOSED.get(p, []):
                        if g >= 0:
                            hidden_low(t, par, g)
                        elif not first:
                            hidden_low(t - 1, 1 - par, g + NG)
                    if p == 1 and not first:
                        result(t - 1, 1 - par, h - (1 - par))
                    if front and p in FRONT:
                        FRONT[p](t + 1, 1 - par, h + par)
                    if first:
                        for n in pieces_of(p):
                            if not by_pool(n):
                                low(n)

            dve.wait_ge(consts_in, 16 * 5)
            nc.vector.memset(any_valid[:, :, 1:2], 0.0)
            nc.vector.tensor_reduce(out=any_valid[:, :, 0:1], in_=mask_in[:, :, :], axis=AX.X, op=ALU.max
                                    ).then_inc(any_valid_made, 1)
            nc.vector.memset(combine[:, :, E:NE], 0.5)
            dve.wait_ge(gate_parts, 1)
            nc.vector.tensor_tensor(Gl[:, :, :], raw_gate[:, :, :], Gh[:, :, :].bitcast(f32), ALU.subtract
                                    ).then_inc(gate_parts, 1)
            for p in sorted(FRONT):
                FRONT[p](0, 0, 0, first=True)
                n = {3: 0, 5: 1, 6: 2, 7: 3}.get(p)
                if n is not None and not by_pool(n):
                    low(n)

            def ending():
                for g in (5, 6):
                    hidden_low(T - 1, 1, g)
                result(T - 1, 1, (T - 2) // 2)

            tiles(dve, step, ending)

        @block.gpsimd
        def _(pool):
            def attention_bias(u):
                if not (isinstance(u, int) and u == 0):
                    pool.wait_ge(scored, u)
                nc.gpsimd.tensor_copy(mask_f[:, 0:P], mask_in[:, bass.ds(u, 1), :].rearrange("b t m -> b (t m)"))
                nc.gpsimd.tensor_copy(bias[:, P:P + 2], any_valid[:, bass.ds(u, 1), :].rearrange("b t m -> b (t m)")
                                      ).then_inc(pool_step, 1)
                pool.wait_ge(pool_step, 1)
                nc.gpsimd.tensor_scalar(bias[:, 0:P], mask_f[:, :], 1.0, -MASKED, ALU.subtract, ALU.mult
                                        ).then_inc(bias_made, 1)
                pool.sem_clear(pool_step)

            def rstd(u, k):
                n = newton[:, k, :]
                pool.wait_ge(moments_made, 2 * u + k + 1)
                nc.gpsimd.tensor_tensor(n[:, 0:1], moments[:, k, 1:2], eps[:, :], ALU.add).then_inc(pool_step, 1)
                pool.wait_ge(pool_step, 1)
                nc.gpsimd.tensor_scalar(n[:, 1:2], n[:, 0:1], -0.5, None, ALU.mult).then_inc(pool_step, 1)
                nc.gpsimd.tensor_scalar(n[:, 2:3].bitcast(i32), n[:, 0:1].bitcast(i32), -0.5, float(0x5f3759df),
                                        ALU.mult, ALU.add).then_inc(pool_step, 1)
                pool.wait_ge(pool_step, 3)
                for k2, (src, dst) in enumerate(((2, 4), (4, 5), (5, 7))):
                    nc.gpsimd.tensor_scalar(n[:, 3:4], n[:, src:src + 1], n[:, src:src + 1], n[:, 1:2],
                                            ALU.mult, ALU.mult).then_inc(pool_step, 1)
                    pool.wait_ge(pool_step, 4 + 2 * k2)
                    last = nc.gpsimd.tensor_scalar(n[:, dst:dst + 1], n[:, 3:4], 1.5, n[:, src:src + 1],
                                                   ALU.add, ALU.mult)
                    if k2 < 2:
                        last.then_inc(pool_step, 1)
                        pool.wait_ge(pool_step, 5 + 2 * k2)
                last.then_inc(rstd_made, 1)
                pool.sem_clear(pool_step)

            def low(n):
                kind, k = PIECES[n]
                pool.wait_ge(high_made, n + 1)
                if kind == "w1":
                    dst, high, cols = W1l[:, k, :, :], W1h[:, k, :, :], WP
                else:
                    c = min(2, NCH - k)
                    dst, high, cols = W2l[:, k:k + c, :], W2h[:, k:k + c, :], c * D
                nc.gpsimd.tensor_tensor(dst.rearrange("p c n -> p (c n)"), raw[:, n % NRAW, 0:cols],
                                        high.bitcast(f32).rearrange("p c n -> p (c n)"), ALU.subtract
                                        ).then_inc(low_by_pool, 1)

            def step(t, par, h, first=False, front=True):
                for p in range(NP):
                    if first:
                        for n in pieces_of(p):
                            if by_pool(n):
                                low(n)
                    if front and p == 0:
                        attention_bias(t + 1)
                        rstd(t + 1, 0)
                    if front and p == 5:
                        rstd(t + 1, 1)

            pool.wait_ge(consts_in, 16 * 5)
            pool.wait_ge(any_valid_made, 1)
            nc.gpsimd.memset(eps[:, :], EPS)
            attention_bias(0)
            rstd(0, 0)
            rstd(0, 1)
            for n in range(FIRST_PIECES):
                if by_pool(n):
                    low(n)
            tiles(pool, step, lambda: None)


def kernel(x, ctx_2048, mask_BxS2_bk0, g_xattn, g_ffn, L0_ffn_gate_w, L0_ffn_w1, L0_ffn_w2,
           L0_ffn_shared_w1, L0_ffn_shared_w2):
    import numpy as np
    import concourse.bacc as bacc
    from concourse.bass_utils import run_bass_kernel_spmd

    c = np.ascontiguousarray
    x, ctx = np.asarray(x).reshape(T * P, D), np.asarray(ctx_2048).reshape(T * P, D)
    ctx_t = c(ctx.reshape(T, P, KC, P).transpose(3, 0, 2, 1))
    mask = np.zeros((BT, T, P), np.uint8)
    bits = np.asarray(mask_BxS2_bk0).view(np.uint8).reshape(T, BT, M)
    for b in range(BT):
        mask[b, :, b * M:(b + 1) * M] = bits[:, b, :]
    mask = mask.view(np.int32)
    gates = c(np.broadcast_to(np.concatenate([np.asarray(g_xattn), np.asarray(g_ffn)])[None, :], (P, 2)))
    gate_w = c(np.asarray(L0_ffn_gate_w).T.reshape(KC, P, E).transpose(1, 0, 2))
    sw1 = np.asarray(L0_ffn_shared_w1).reshape(2, SH, I, D).transpose(1, 0, 2, 3).reshape(SH, 2 * I, D)
    w1 = np.concatenate([np.asarray(L0_ffn_w1), sw1])
    w1 = c(w1.reshape(NE, 2 * I, KC, P).transpose(0, 3, 2, 1).reshape(NE, P, WP))
    w2 = np.concatenate([np.asarray(L0_ffn_w2).transpose(0, 2, 1).reshape(E * I, D), np.asarray(L0_ffn_shared_w2).T])
    w2 = np.concatenate([w2, np.zeros((NCH * P - HID, D), w2.dtype)])
    w2 = c(w2.reshape(NCH, P, D).transpose(1, 0, 2).reshape(P, NCH * D))
    ident = np.eye(P, dtype=np.float32)
    sel = c(np.repeat(np.eye(BT, dtype=np.float32), S, axis=1))

    arrays = {"x": x, "ctx_n": ctx, "ctx_t": ctx_t, "mask": mask, "gates": gates, "gate_w": gate_w,
              "w1": w1, "w2": w2, "ident": ident, "sel": sel}
    nc = bacc.Bacc("TRN2", target_bir_lowering=False, num_devices=1)
    args = {k: nc.dram_tensor("in_" + k, a.shape, mybir.dt.from_np(a.dtype), kind="ExternalInput").ap()
            for k, a in arrays.items()}
    out = nc.dram_tensor("out", (T * P, D), mybir.dt.float32, kind="ExternalOutput").ap()
    gated_flamingo_block(nc, out=out, **args)
    r = run_bass_kernel_spmd(nc, [{"in_" + k: c(a) for k, a in arrays.items()}], core_ids=[0])
    return r.results[0]["out"].reshape(B, S, D)
```

```python
from contextlib import ExitStack

import concourse.bass as bass
from concourse import mybir

B, S, M, D = 32, 64, 64, 256
P = 128
N = B * S
T = N // P
BT = P // S
KC = D // P
G = 4
NGRP = T // G
GT = G * P
E, I, TOPK = 16, 176, 6
IC = 2
IR = I // IC
SI = 352
SC = -(-SI // P)
W1C = KC * 2 * I
ROW = D + E
U = 8
R = 4
SLOT_TILES = (TOPK * N + E * (P - 1)) // P
ST = -(-SLOT_TILES // U) * U
EPS = 1e-5
MASKED = -1e30 * D ** 0.5
AHEAD = 3

C_IDENT, C_IOTA, C_TRI, C_K128, C_ID1, C_PAD, C_END = 0, 128, 256, 384, 400, 416, 417
HOT = 4


def srows(c):
    return min(P, SI - c * P)


def sparse_block(nc, x, ctx_n, ctx_t, mask, gates, gate_w, w1, w1s, w2, w2s, consts, sel, out):
    f32, f32r, f16 = mybir.dt.float32, mybir.dt.float32r, mybir.dt.float16
    u8, i32, u32 = mybir.dt.uint8, mybir.dt.int32, mybir.dt.uint32
    ALU, ACT, AX = mybir.AluOpType, mybir.ActivationFunctionType, mybir.AxisListType

    rows_dram = nc.dram_tensor("rows_dram", (N + P, ROW), f32, kind="Internal").ap()
    sums = [nc.dram_tensor(f"sum_{k}", (N + P, D), f32, kind="Internal").ap() for k in "xy"]

    with ExitStack() as stack:
        def sem(name):
            return stack.enter_context(nc.semaphore(name))

        def allocator(s):
            return lambda name, shape, dt=f32: s.enter_context(nc.sbuf_tensor(name, shape, dt))

        sb = allocator(stack)
        W1h, W1l = sb("W1h", [P, E, KC, 2 * I], f32r), sb("W1l", [P, E, KC, 2 * I], f32r)
        const = sb("const", [P, C_END])
        gates_in, gate_tanh, half_tanh = sb("gates_in", [P, 2]), sb("gate_tanh", [P, 2]), sb("half_tanh", [P, 1])
        rows = sb("rows", [P, G, ROW])
        xTh, xTl = sb("xTh", [P, KC * GT], f32r), sb("xTl", [P, KC * GT], f32r)
        y = sb("y", [P, G, D])
        chosen = sb("chosen", [P, T, E], f16)
        slot_ids = sb("slot_ids", [P, ST], u32)
        tile_expert = sb("tile_expert", [1, ST], i32)
        gather_ids, scatter_ids = sb("gather_ids", [P, R], u32), sb("scatter_ids", [P, R], u32)
        iotas, tri = sb("iotas", [P, P, TOPK], f16), sb("tri", [P, P], f16)
        ones, zeros16 = sb("ones", [P, P], f16), sb("zeros16", [P, (T + 1) * E], f16)
        tiles_of, expert_of = sb("tiles_of", [P, E]), sb("expert_of", [P, 2])
        prefix = sb("prefix", [P, 2, 8 + E])
        wide = sb("wide", [P, 2, T * E])
        base = sb("base", [P, 2, E])
        places = sb("places", [P, T, 8])
        place_bits = sb("place_bits", [P, 3, T * 8], i32)
        tile_no, slot_no = sb("tile_no", [P, T, 8], f16), sb("slot_no", [P, T, 8], f16)

        first = ExitStack()
        sb = allocator(first)
        RAWC = max(W1C, SC * D)
        raw = sb("raw", [P, 4, RAWC])
        ctx_in, ctxT_in = sb("ctx_in", [P, G, D]), sb("ctxT_in", [P, G, KC, P])
        W1sh, W1sl = sb("W1sh", [P, KC, 2 * SI], f32r), sb("W1sl", [P, KC, 2 * SI], f32r)
        W2sh, W2sl = sb("W2sh", [P, SC, D], f32r), sb("W2sl", [P, SC, D], f32r)
        gate_parts_r = sb("gate_parts_r", [P, KC, 2, E], f32r)
        Gh, Gl = gate_parts_r[:, :, 0, :], gate_parts_r[:, :, 1, :]
        raw_gate = sb("raw_gate", [P, KC, E])
        mask_words = sb("mask_words", [BT, T, P // 4], i32)
        mask_in = mask_words[:, :, :].bitcast(u8)
        any_valid, selector = sb("any_valid", [BT, T]), sb("selector", [BT, P])
        bias, selector_r = sb("bias", [BT, T, P], f32r), sb("selector_r", [BT, P], f32r)
        valid_gate = sb("valid_gate", [P, T])
        x_in = sb("x_in", [P, 2, G, D])
        xn, xnT = sb("xn", [P, G, D]), sb("xnT", [P, G, KC, P])
        stats, moments = sb("stats", [P, 2, G, 6]), sb("moments", [P, 2, G, 2])
        newton, eps = sb("newton", [P, 2, 8, G]), sb("eps", [P, G])
        small = sb("small", [P, 8, G])
        probs, probsT = sb("probs", [P, G, P]), sb("probsT", [P, G, P])
        router = sb("router", [P, 3, G, E])
        rsmall = sb("rsmall", [P, 4, G])
        top8 = sb("top8", [P, G, 8])
        act_s = sb("act_s", [P, 2, GT])
        hsh, hsl = sb("hsh", [P, SC, GT], f32r), sb("hsl", [P, SC, GT], f32r)
        zero = sb("zero", [P, ROW])
        first.close()

        HOT_BYTES = 2 * HOT * TOPK * (P + 2 * ST)
        hot = ExitStack()
        sb = allocator(hot)
        hot_slot = sb("hot_slot", [P, HOT, P, TOPK], f16)
        hot_tile01 = sb("hot_tile01", [P, HOT, ST, TOPK], f16)
        hot_tile = sb("hot_tile", [P, HOT, ST, TOPK], f16)
        hot.close()

        later = ExitStack()
        sb = allocator(later)
        gated, hidden = sb("gated", [P, 2, I]), sb("hidden", [P, 2, I])
        hTh, hTl = sb("hTh", [IR, 2, IC, P], f32r), sb("hTl", [IR, 2, IC, P], f32r)
        sb("hot_rest", [P, HOT_BYTES // 4 - 4 * I - 4 * IC * P])
        W2h, W2l = sb("W2h", [IR, E, IC, D], f32r), sb("W2l", [IR, E, IC, D], f32r)
        raw2 = sb("raw2", [IR, 2, 2, IC * D])
        later.close()

        last = ExitStack()
        sb = allocator(last)
        part = sb("part", [P, 2, 2, G, D])
        last.close()

        bank = stack.enter_context(nc.psum_tensor("bank", [P, 8, 512], f32))
        xnT_ps = bank[:, 0:2, :].rearrange("p b (t c n) -> p (b t) c n", t=2, c=KC)
        read_ps = bank[:, 0:2, :].rearrange("p b (t n) -> p (b t) n", t=2)
        score_ps = bank[:, 2, :].rearrange("p (t n) -> p t n", t=G)
        x2T_ps = [bank[:, b, :].rearrange("p (t c n) -> p t c n", t=2, c=KC) for b in (7, 2)]
        logit_ps = bank[:, 3, 0:G * 2 * E].rearrange("p (t q e) -> p t q e", t=G, q=2)
        outs_ps = [bank[:, b, :].rearrange("p (t n) -> p t n", t=2) for b in (3, 6)]
        gate_ps, up_ps = [bank[:, 4, :], bank[:, 6, :]], [bank[:, 5, :], bank[:, 7, :]]
        valid_ps = bank[:, 7, 0:T]
        rank_ps = bank[:, 0, 0:(T + 1) * E].rearrange("p (t e) -> p t e", e=E)
        inverse_ps = bank[:, 1, 0:ST]
        expert_ps = bank[0:1, 2, 0:P]
        gT_ps, gu_ps, hT_ps, y_ps = bank[:, 0:2, :], bank[:, 2:4, :], bank[:, 4:6, :], bank[:, 6:8, :]

        consts_in, x_arrived, ctx_arrived = sem("consts_in"), sem("x_arrived"), sem("ctx_arrived")
        raw_in = [sem(f"raw_in_{k}") for k in range(4)]
        raw2_in = [sem(f"raw2_in_{k}") for k in range(2)]
        x2_stored, rows_stored, pads_stored = sem("x2_stored"), sem("rows_stored"), sem("pads_stored")
        shared_stored = [sem("shared_stored_0"), sem("shared_stored_1")]
        gates_made, valid_reduced, valid_spread, valid_made, bias_made, routing_consts, zero_made, gate_parts = (
            sem("gates_made"), sem("valid_reduced"), sem("valid_spread"), sem("valid_made"), sem("bias_made"),
            sem("routing_consts"), sem("zero_made"), sem("gate_parts"))
        high_made, low_made = sem("high_made"), sem("low_made")
        gather_ids_made, scatter_ids_made = sem("gather_ids_made"), sem("scatter_ids_made")
        dma_allowed = sem("dma_allowed")
        high2_made, low2_made = sem("high2_made"), sem("low2_made")
        moments_made = [sem("moments_made"), sem("moments2_made")]
        rstd_made = [sem("rstd_made"), sem("rstd2_made")]
        xn_made, xnT_done, xnT_made = sem("xn_made"), sem("xnT_done"), sem("xnT_made")
        scored, max_made, exp_made = sem("scored"), sem("max_made"), sem("exp_made")
        probsT_done, probsT_made, readout_done = sem("probsT_done"), sem("probsT_made"), sem("readout_done")
        x2n_made = sem("x2n_made")
        x2T_done, xTh_made, xTl_made = sem("x2T_done"), sem("xTh_made"), sem("xTl_made")
        logits_done, logits_shifted, route_exp, weights_made = (
            sem("logits_done"), sem("logits_shifted"), sem("route_exp"), sem("weights_made"))
        s_up_done, s_tanh_made, s_act_made, s_high_made, s_low_made = (
            sem("s_up_done"), sem("s_tanh_made"), sem("s_act_made"), sem("s_high_made"), sem("s_low_made"))
        s_down_done, s_out_made = sem("s_down_done"), sem("s_out_made")
        ranked, places_made = sem("ranked"), sem("places_made")
        hot_made, hot_scaled, hot_used = (
            sem("hot_made"), sem("hot_scaled"), sem("hot_used"))
        ids_made, expert_counted, expert_turned, expert_made = (
            sem("ids_made"), sem("expert_counted"), sem("expert_turned"), sem("expert_made"))
        vector_step, pool_step = sem("vector_step"), sem("pool_step")
        gathered = [sem(f"gathered_{k}") for k in range(R)]
        scattered = [sem(f"scattered_{k}") for k in range(R)]
        c_xT_done, c_xTh_made, c_xTl_made = sem("c_xT_done"), sem("c_xTh_made"), sem("c_xTl_made")
        c_up_done, c_tanh_made, c_gated_made, c_hidden_made = (
            sem("c_up_done"), sem("c_tanh_made"), sem("c_gated_made"), sem("c_hidden_made"))
        c_hT_done, c_hTh_made, c_hTl_made, c_down_done, c_y_made = (
            sem("c_hT_done"), sem("c_hTh_made"), sem("c_hTl_made"), sem("c_down_done"), sem("c_y_made"))
        parts_in = [sem("parts_in_0"), sem("parts_in_1")]
        summed, out_stored = sem("summed"), sem("out_stored")

        block = stack.enter_context(nc.Block())
        identity = const[:, C_IDENT:C_IDENT + P]

        def wait(eng, s, value):
            if not (isinstance(value, int) and value <= 0):
                eng.wait_ge(s, value)

        def groups(eng, body):
            body(0)
            with eng.Fori(1, NGRP - 2) as n:
                body(n)
            body(NGRP - 2, front=False)

        def slot_tiles(eng, step, turn=None):
            turn = turn or (lambda i: None)
            experts = turn(0)
            for k in range(U):
                step(k, k, 0, experts)
            with eng.Fori(1, ST // U - 1) as i:
                experts = turn(i)
                for k in range(U):
                    step(i * U + k, k, i, experts)
            experts = turn(ST // U - 1)
            for j in range(ST - U, ST + AHEAD):
                step(j, j % U, j // U, experts)

        turns_made = [0]

        def turn_experts(eng, i, before):
            turns_made[0] += 1
            regs = [eng.alloc_register(f"expert_{turns_made[0]}_{q}") for q in range(before + U)]
            eng.load(regs, tile_expert[0:1, bass.ds(i * U - before, len(regs))])
            return {q - before: bass.RuntimeValue.of_register_unchecked(reg, min_val=0, max_val=E - 1)
                    for q, reg in enumerate(regs)}

        def high2(act, q):
            act.wait_ge(raw2_in[q % 2], 16 * (q // 2 + 1))
            nc.scalar.copy(W2h[:, 2 * q:2 * q + 2, :, :].rearrange("p e c n -> p (e c n)"),
                           raw2[:, q % 2, :, :].rearrange("p e n -> p (e n)")).then_inc(high2_made, 1)

        @block.sync
        def _(sp):
            def load_x(g):
                wait(sp, moments_made[0], g)
                wait(sp, x2_stored, (g - 1) * 16)
                wait(sp, x2n_made, g - 1)
                sp.dma_start(x_in[:, g % 2, :, :],
                             x[bass.ds(g * GT, GT), :].rearrange("(t p) d -> p t d", p=P)).then_inc(x_arrived, 16)

            def load_ctx(g):
                wait(sp, moments_made[1], g)
                sp.dma_start(ctxT_in[:, :, :, :], ctx_t[:, bass.ds(g * G, G), :, :]).then_inc(ctx_arrived, 16)
                sp.dma_start(ctx_in[:, :, :], ctx_n[bass.ds(g * GT, GT), :].rearrange("(t p) d -> p t d", p=P)
                             ).then_inc(ctx_arrived, 16)

            def load_piece(k, src, cols, made):
                wait(sp, low_made, made)
                sp.dma_start(raw[:, k, 0:cols], src).then_inc(raw_in[k], 16)

            def store_x2(g):
                sp.wait_ge(moments_made[1], g + 1)
                sp.dma_start(sums[0][bass.ds(g * GT, GT), :].rearrange("(t p) d -> p t d", p=P),
                             x_in[:, g % 2, :, :]).then_inc(x2_stored, 16)

            def store_rows(g):
                sp.wait_ge(weights_made, g + 1)
                sp.dma_start(rows_dram[bass.ds(g * GT, GT), :].rearrange("(t p) d -> p t d", p=P),
                             rows[:, :, :]).then_inc(rows_stored, 16)

            def store_shared(g, h):
                sp.wait_ge(s_out_made, 2 * g + h + 1)
                sp.dma_start(sums[1][bass.ds(g * GT + h * 2 * P, 2 * P), :].rearrange("(t p) d -> p t d", p=P),
                             y[:, 2 * h:2 * h + 2, :]).then_inc(shared_stored[h], 16)

            load_x(0)
            for dst, src in ((const[:, :], consts), (mask_words[:, :, :], mask), (selector[:, :], sel),
                             (gates_in[:, :], gates), (raw_gate[:, :, :], gate_w)):
                sp.dma_start(dst, src).then_inc(consts_in, 16)
            load_ctx(0)
            load_x(1)
            load_piece(0, w1s[:, 0, :], 2 * SI, 0)
            load_piece(1, w1s[:, 1, :], 2 * SI, 0)
            load_piece(2, w2s[:, :], SC * D, 0)
            for k in range(4):
                load_piece((3 + k) % 4, w1[k, :, :], W1C, k)
            sp.wait_ge(zero_made, 1)
            sp.dma_start(rows_dram[N:N + P, :], zero[:, :]).then_inc(pads_stored, 16)
            for s in sums:
                sp.dma_start(s[N:N + P, :], zero[:, 0:D]).then_inc(pads_stored, 16)
            store_x2(0)
            load_ctx(1)

            def body(n):
                if n + 2 < NGRP:
                    load_x(n + 2)
                for k in range(4):
                    sp.wait_ge(low_made, n * 4 + 4 + k)
                    sp.dma_start(raw[:, (3 + k) % 4, 0:W1C], w1[n * 4 + 4 + k, :, :]).then_inc(raw_in[(3 + k) % 4], 16)
                store_rows(n)
                store_x2(n + 1)
                if n + 2 < NGRP:
                    load_ctx(n + 2)
                store_shared(n, 0)
                store_shared(n, 1)

            for n in range(NGRP - 1):
                body(n)
            store_rows(3)
            store_shared(3, 0)
            store_shared(3, 1)
            sp.wait_ge(s_down_done, 2 * NGRP)
            for q in range(E // 2):
                if q >= 2:
                    sp.wait_ge(low2_made, q - 1)
                sp.dma_start(raw2[:, q % 2, :, :], w2[:, 2 * q:2 * q + 2, :]).then_inc(raw2_in[q % 2], 16)
            for k in range(R):
                sp.wait_ge(scattered[k], 16 * (ST // R))
            for g in range(NGRP):
                if g >= 2:
                    sp.wait_ge(out_stored, 16 * (g - 1))
                for a in range(2):
                    sp.dma_start(part[:, g % 2, a, :, :],
                                 sums[a][g * GT:(g + 1) * GT, :].rearrange("(t p) d -> p t d", p=P)
                                 ).then_inc(parts_in[g % 2], 16)
                if g >= 1:
                    sp.wait_ge(summed, g)
                    sp.dma_start(out[(g - 1) * GT:g * GT, :].rearrange("(t p) d -> p t d", p=P),
                                 part[:, (g - 1) % 2, 0, :, :]).then_inc(out_stored, 16)
            sp.wait_ge(summed, NGRP)
            sp.dma_start(out[(NGRP - 1) * GT:, :].rearrange("(t p) d -> p t d", p=P),
                         part[:, (NGRP - 1) % 2, 0, :, :]).then_inc(out_stored, 16)
            sp.wait_ge(out_stored, 16 * NGRP)

        @block.tensor
        def _(pe):
            def split_product(dst, lh, ll, rh, rl, start, stop):
                nc.tensor.matmul(dst, lh, rh, start=start, stop=False)
                nc.tensor.matmul(dst, lh, rl, start=False, stop=False)
                return nc.tensor.matmul(dst, ll, rh, start=False, stop=stop)

            def transpose_xn(g):
                pe.wait_ge(xn_made, g + 1)
                wait(pe, moments_made[1], g)
                for t in range(G):
                    for c in range(KC):
                        end = nc.tensor.transpose(xnT_ps[:, t, c, :], xn[:, t, c * P:(c + 1) * P], identity)
                end.then_inc(xnT_done, 1)

            def scores(g):
                pe.wait_ge(ctx_arrived, g * 32 + 32)
                pe.wait_ge(xnT_made, g + 1)
                for t in range(G):
                    nc.tensor.matmul(score_ps[:, t, :], selector_r[:, :],
                                     bias[:, bass.ds(g * G + t, 1), :].rearrange("b t m -> b (t m)"),
                                     start=True, stop=False)
                    for c in range(KC):
                        end = nc.tensor.matmul(score_ps[:, t, :], xnT[:, t, c, :], ctxT_in[:, t, c, :],
                                               start=False, stop=c == KC - 1)
                end.then_inc(scored, 1)

            def transpose_probs(g):
                pe.wait_ge(exp_made, g + 1)
                for t in range(G):
                    end = nc.tensor.transpose(score_ps[:, t, :], probs[:, t, :], identity)
                end.then_inc(probsT_done, 1)

            def readout(g):
                pe.wait_ge(probsT_made, g + 1)
                for t in range(G):
                    end = nc.tensor.matmul(read_ps[:, t, :], probsT[:, t, :], ctx_in[:, t, :], start=True, stop=True)
                end.then_inc(readout_done, 1)

            def transpose_x2n(g, h):
                pe.wait_ge(x2n_made, g + 1)
                pe.wait_ge(probsT_made, g + 1)
                wait(pe, s_act_made, 3 * g - 1)
                for t in range(2):
                    for c in range(KC):
                        end = nc.tensor.transpose(x2T_ps[h][:, t, c, :], rows[:, 2 * h + t, c * P:(c + 1) * P], identity)
                end.then_inc(x2T_done, 1)

            def logits(g):
                pe.wait_ge(xTl_made, 2 * g + 2)
                wait(pe, s_out_made, 2 * g - 1)
                for t in range(G):
                    for n, (a, c) in enumerate((a, c) for a in (xTh, xTl) for c in range(KC)):
                        end = nc.tensor.matmul(logit_ps[:, t, :, :], a[:, c * GT + t * P:c * GT + (t + 1) * P],
                                               gate_parts_r[:, c, :, :], start=n == 0, stop=n == 2 * KC - 1)
                end.then_inc(logits_done, 1)

            def shared_up(g, c, parts=(0, 1)):
                pe.wait_ge(xTl_made, 2 * g + 2)
                if c == 1:
                    wait(pe, s_out_made, 2 * g)
                wait(pe, s_act_made, 3 * g + c - 1)
                r = srows(c)
                for dst, at in [((gate_ps[c % 2], 0), (up_ps[c % 2], SI))[q] for q in parts]:
                    for k in range(KC):
                        a = slice(at + c * P, at + c * P + r)
                        tok = slice(k * GT, (k + 1) * GT)
                        end = split_product(dst[0:r, :], W1sh[:, k, a], W1sl[:, k, a], xTh[:, tok], xTl[:, tok],
                                            k == 0, k == KC - 1)
                if 1 in parts:
                    end.then_inc(s_up_done, 1)

            def shared_down(g, h):
                pe.wait_ge(s_low_made, 3 * g + 3)
                if h == 0:
                    pe.wait_ge(route_exp, g + 1)
                else:
                    pe.wait_ge(s_act_made, 3 * g + 2)
                for t in range(2):
                    for c in range(SC):
                        r, tok = srows(c), slice((2 * h + t) * P, (2 * h + t + 1) * P)
                        end = split_product(outs_ps[h][:, t, :], hsh[0:r, c, tok], hsl[0:r, c, tok],
                                            W2sh[0:r, c, :], W2sl[0:r, c, :], c == 0, c == SC - 1)
                end.then_inc(s_down_done, 1)

            pe.wait_ge(consts_in, 16 * 5)
            pe.wait_ge(valid_reduced, 1)
            nc.tensor.matmul(valid_ps, selector[:, :], any_valid[:, :], start=True, stop=True).then_inc(valid_spread, 1)

            transpose_xn(0)
            pe.wait_ge(bias_made, 1)
            pe.wait_ge(gate_parts, 2)
            scores(0)
            transpose_probs(0)
            readout(0)
            transpose_xn(1)
            pe.wait_ge(valid_made, 1)
            def body(n, front=True):
                shared_up(n, 0)
                logits(n)
                scores(n + 1)
                shared_up(n, 1, (0,))
                transpose_probs(n + 1)
                shared_up(n, 1, (1,))
                readout(n + 1)
                shared_up(n, 2)
                if front:
                    transpose_xn(n + 2)
                transpose_x2n(n + 1, 0)
                transpose_x2n(n + 1, 1)
                shared_down(n, 0)
                shared_down(n, 1)

            transpose_x2n(0, 0)
            transpose_x2n(0, 1)
            pe.wait_ge(low_made, 3)
            groups(pe, body)
            n = NGRP - 1
            shared_up(n, 0)
            logits(n)
            shared_up(n, 1, (0,))

            pe.wait_ge(routing_consts, 1)
            pe.wait_ge(weights_made, NGRP)
            nc.tensor.matmul(bank[:, 0, 0:(T + 1) * E], ones[:, :], zeros16[:, :], start=True, stop=False)
            nc.tensor.matmul(bank[:, 0, 0:T * E], tri[:, :], chosen[:, :, :].rearrange("p t e -> p (t e)"),
                             start=False, stop=False)
            for t in range(T):
                later_tiles = chosen[:, t:t + 1, :].to_broadcast([P, T - t, E])
                end = nc.tensor.matmul(rank_ps[:, t + 1:T + 1, :], ones[:, :], later_tiles,
                                       start=False, stop=t == T - 1)
            end.then_inc(ranked, 1)
            shared_up(n, 1, (1,))
            shared_up(n, 2)
            shared_down(n, 0)
            shared_down(n, 1)
            pe.wait_ge(expert_counted, 1)
            nc.tensor.matmul(expert_ps, expert_of[:, 1:2], identity, start=True, stop=True).then_inc(expert_turned, 1)

            for t in range(T):
                pe.wait_ge(hot_scaled, t + 1)
                for r in range(TOPK):
                    end = nc.tensor.matmul(inverse_ps, hot_slot[:, t % HOT, :, r], hot_tile[:, t % HOT, :, r],
                                           start=t == 0 and r == 0, stop=t == T - 1 and r == TOPK - 1)
                end.then_inc(hot_used, 1)

            def step(j, k, i, experts):
                static = isinstance(j, int)

                def transpose_rows(j1, k1, i1):
                    pe.wait_ge(gathered[k1], i1 * 16 + 16)
                    wait(pe, c_xTl_made, j1 - 1)
                    for c in range(KC):
                        end = nc.tensor.transpose(gT_ps[:, k1 % 2, c * P:(c + 1) * P],
                                                  rows[:, k1 % R, c * P:(c + 1) * P], identity)
                    end.then_inc(c_xT_done, 1)

                if static and j == 0:
                    transpose_rows(0, 0, 0)
                if not static or j + 1 < ST:
                    transpose_rows(j + 1, (k + 1) % R, i * (U // R) + (k + 1) // R)
                if not static or j < ST:
                    e = experts[k]
                    pe.wait_ge(c_xTl_made, j + 1)
                    wait(pe, c_hidden_made, j - 1)
                    for c in range(KC):
                        at = slice((k % 2) * 2 * P + c * P, (k % 2) * 2 * P + (c + 1) * P)
                        end = split_product(gu_ps[:, k % 2, 0:2 * I], xTh[:, at], xTl[:, at],
                                            W1h[:, bass.ds(e, 1), c, :].rearrange("p e n -> p (e n)"),
                                            W1l[:, bass.ds(e, 1), c, :].rearrange("p e n -> p (e n)"),
                                            c == 0, c == KC - 1)
                    end.then_inc(c_up_done, 1)
                if static and j == 1:
                    pe.wait_ge(low2_made, E // 2)
                if (not static) or 1 <= j <= ST:
                    k1 = (k - 1) % R
                    pe.wait_ge(c_hidden_made, j)
                    wait(pe, c_hTl_made, j - 2)
                    for c in range(IC):
                        end = nc.tensor.transpose(hT_ps[0:IR, k1 % 2, c * P:(c + 1) * P],
                                                  hidden[:, k1 % 2, c * IR:(c + 1) * IR], identity)
                    end.then_inc(c_hT_done, 1)
                if (not static) or 2 <= j <= ST + 1:
                    k2 = (k - 2) % R
                    e = experts[j - 2 - (ST - U)] if static and j >= ST else experts[k - 2]
                    pe.wait_ge(c_hTl_made, j - 1)
                    wait(pe, c_y_made, j - 3)
                    for c in range(IC):
                        end = split_product(y_ps[:, k2 % 2, 0:D], hTh[:, k2 % 2, c, :], hTl[:, k2 % 2, c, :],
                                            W2h[:, bass.ds(e, 1), c, :].rearrange("p e n -> p (e n)"),
                                            W2l[:, bass.ds(e, 1), c, :].rearrange("p e n -> p (e n)"),
                                            c == 0, c == IC - 1)
                    end.then_inc(c_down_done, 1)

            pe.wait_ge(expert_made, 1)
            pe.wait_ge(ids_made, 1)
            pe.wait_ge(s_out_made, 2 * NGRP)
            slot_tiles(pe, step, lambda i: turn_experts(pe, i, 0 if isinstance(i, int) and i == 0 else R))

        @block.scalar
        def _(act):
            def copy_xnT(g):
                act.wait_ge(xnT_done, g + 1)
                nc.scalar.copy(xnT[:, :, :, :].rearrange("p t c n -> p (t c n)"),
                               bank[:, 0:2, :].rearrange("p b n -> p (b n)")).then_inc(xnT_made, 1)

            def exp_scores(g):
                act.wait_ge(max_made, g + 1)
                for t in range(G):
                    end = nc.scalar.activation(probs[:, t, :], score_ps[:, t, :], ACT.Exp, bias=small[:, 1, t:t + 1],
                                               scale=D ** -0.5, accum_out=small[:, 2, t:t + 1])
                end.then_inc(exp_made, 1)

            def copy_probsT(g):
                act.wait_ge(probsT_done, g + 1)
                nc.scalar.copy(probsT[:, :, :].rearrange("p t n -> p (t n)"), bank[:, 2, :]).then_inc(probsT_made, 1)

            def high_x2n(g, h):
                act.wait_ge(x2T_done, 2 * g + h + 1)
                nc.scalar.copy(xTh[:, :].rearrange("p (c t n) -> p t c n", c=KC, t=G)[:, 2 * h:2 * h + 2, :, :],
                               x2T_ps[h]).then_inc(xTh_made, 1)

            def exp_logits(g):
                act.wait_ge(logits_shifted, g + 1)
                nc.scalar.activation(router[:, 0, :, :], router[:, 1, :, :], ACT.Exp).then_inc(route_exp, 1)

            def shared_tanh(g, c):
                act.wait_ge(s_up_done, 3 * g + c + 1)
                wait(act, s_low_made, 3 * g + c - (1 if c else 0))
                r = srows(c)
                nc.scalar.activation(act_s[0:r, c % 2, :], gate_ps[c % 2][0:r, :], ACT.Tanh, scale=0.5
                                     ).then_inc(s_tanh_made, 1)

            def shared_high(g, c):
                act.wait_ge(s_act_made, 3 * g + c + 1)
                if c == 0:
                    wait(act, s_down_done, 2 * g)
                r = srows(c)
                nc.scalar.copy(hsh[0:r, c, :], act_s[0:r, c % 2, :]).then_inc(s_high_made, 1)

            def shared_out(g, h):
                act.wait_ge(s_down_done, 2 * g + h + 1)
                wait(act, shared_stored[h], g * 16)
                nc.scalar.copy(y[:, 2 * h:2 * h + 2, :], outs_ps[h]).then_inc(s_out_made, 1)

            def high(k, dst, cols, value):
                act.wait_ge(raw_in[k], value)
                nc.scalar.copy(dst, raw[:, k, 0:cols]).then_inc(high_made, 1)

            def high_expert(e, k, value):
                high(k, W1h[:, bass.ds(e, 1), :, :].rearrange("p e c n -> p (e c n)"), W1C, value)

            act.wait_ge(consts_in, 16 * 5)
            nc.scalar.activation(gate_tanh[:, :], gates_in[:, :], ACT.Tanh).then_inc(gates_made, 1)
            nc.scalar.copy(Gh, raw_gate[:, :, :])
            nc.scalar.copy(selector_r[:, :], selector[:, :]).then_inc(gate_parts, 1)
            copy_xnT(0)
            high(0, W1sh[:, 0, :], 2 * SI, 16)
            high(1, W1sh[:, 1, :], 2 * SI, 16)
            exp_scores(0)
            copy_probsT(0)
            copy_xnT(1)
            high(2, W2sh[:, :, :].rearrange("p c n -> p (c n)"), SC * D, 16)
            high_expert(0, 3, 16)

            def body(n, front=True):
                def expert(k):
                    high_expert(n * 4 + 4 + k, (3 + k) % 4, n * 16 + (32 if k == 0 else 48))

                shared_tanh(n, 0)
                shared_high(n, 0)
                exp_logits(n)
                exp_scores(n + 1)
                copy_probsT(n + 1)
                shared_tanh(n, 1)
                shared_high(n, 1)
                expert(0)
                expert(1)
                shared_tanh(n, 2)
                if front:
                    copy_xnT(n + 2)
                shared_high(n, 2)
                high_x2n(n + 1, 0)
                high_x2n(n + 1, 1)
                expert(2)
                shared_out(n, 0)
                expert(3)
                shared_out(n, 1)

            high_x2n(0, 0)
            high_x2n(0, 1)
            for k in range(1, 4):
                high_expert(k, (3 + k) % 4, 32)
            groups(act, body)
            n = NGRP - 1
            shared_tanh(n, 0)
            shared_high(n, 0)
            exp_logits(n)
            for c in (1, 2):
                shared_tanh(n, c)
                shared_high(n, c)

            def scale_hot(t):
                act.wait_ge(hot_made, t + 1)
                if t >= HOT:
                    act.wait_ge(hot_used, t - HOT + 1)
                nc.scalar.activation(hot_tile[:, t % HOT, :, :], hot_tile01[:, t % HOT, :, :], ACT.Copy,
                                     scale=const[:, C_ID1 + t:C_ID1 + t + 1]).then_inc(hot_scaled, 1)

            scale_hot(0)
            shared_out(n, 0)
            scale_hot(1)
            shared_out(n, 1)
            act.wait_ge(expert_turned, 1)
            nc.scalar.copy(tile_expert[:, :], expert_ps[:, 0:ST]).then_inc(expert_made, 1)

            for t in range(2, T):
                scale_hot(t)
                if t % 2:
                    high2(act, t // 2 - 1)
            high2(act, T // 2 - 1)

            def step(j, k, i, experts):
                static = isinstance(j, int)

                def high_rows(j1, k1):
                    act.wait_ge(c_xT_done, j1 + 1)
                    nc.scalar.copy(xTh[:, (k1 % 2) * 2 * P:(k1 % 2 + 1) * 2 * P], gT_ps[:, k1 % 2, 0:2 * P]
                                   ).then_inc(c_xTh_made, 1)

                if static and j == 0:
                    high_rows(0, 0)
                if not static or j + 1 < ST:
                    high_rows(j + 1, k + 1)
                if not static or j < ST:
                    act.wait_ge(c_up_done, j + 1)
                    nc.scalar.activation(gated[:, k % 2, :], gu_ps[:, k % 2, 0:I], ACT.Tanh, scale=0.5
                                         ).then_inc(c_tanh_made, 1)
                if (not static) or 1 <= j <= ST:
                    act.wait_ge(c_hT_done, j)
                    nc.scalar.copy(hTh[:, (k - 1) % 2, :, :], hT_ps[0:IR, (k - 1) % 2, 0:IC * P].rearrange(
                        "p (c n) -> p c n", c=IC)).then_inc(c_hTh_made, 1)
                if (not static) or 2 <= j <= ST + 1:
                    k2 = (k - 2) % R
                    act.wait_ge(c_down_done, j - 1)
                    wait(act, scattered[k2], (i * (U // R) + (k - 2) // R) * 16)
                    nc.scalar.copy(y[:, k2, :], y_ps[:, k2 % 2, 0:D]).then_inc(c_y_made, 1)

            act.wait_ge(shared_stored[0], 16 * NGRP)
            act.wait_ge(shared_stored[1], 16 * NGRP)
            slot_tiles(act, step)

        @block.vector
        def _(dve):
            def chained(ins, value):
                ins.then_inc(vector_step, 1)
                dve.wait_ge(vector_step, value)

            def chain_over():
                dve.sem_clear(vector_step)

            def shared_low(g, c):
                dve.wait_ge(s_high_made, 3 * g + c + 1)
                r = srows(c)
                nc.vector.tensor_tensor(hsl[0:r, c, :], act_s[0:r, c % 2, :], hsh[0:r, c, :].bitcast(f32),
                                        ALU.subtract).then_inc(s_low_made, 1)

            def x_tile(g, t):
                return x_in[:, bass.ds(g % 2, 1), t, :].rearrange("p g d -> p (g d)")

            def moments_of(k, g):
                first = 2 if k else 1
                for t in range(G):
                    end = nc.vector.bn_stats(stats[:, k, t, :],
                                             x_tile(g, t))
                chained(end, first)
                for t in range(G):
                    end = nc.vector.bn_aggr(moments[:, k, t, :], stats[:, k, t, :])
                end.then_inc(moments_made[k], 1)
                chain_over()

            def rstd_here(g, k):
                n = newton[:, k, :, :]
                dve.wait_ge(moments_made[k], g + 1)
                chained(nc.vector.tensor_scalar(n[:, 0, :], moments[:, k, :, 1], EPS, None, ALU.add), 1)
                nc.vector.tensor_scalar(n[:, 1, :], n[:, 0, :], -0.5, None, ALU.mult)
                chained(nc.vector.tensor_scalar(n[:, 2, :].bitcast(i32), n[:, 0, :].bitcast(i32), -0.5,
                                                float(0x5f3759df), ALU.mult, ALU.add), 2)
                for q, (src, dst) in enumerate(((2, 5), (5, 6), (6, 7))):
                    chained(nc.vector.tensor_tensor(n[:, 3, :], n[:, src, :], n[:, src, :], ALU.mult), 3 + 3 * q)
                    chained(nc.vector.tensor_tensor(n[:, 4, :], n[:, 3, :], n[:, 1, :], ALU.mult), 4 + 3 * q)
                    end = nc.vector.scalar_tensor_tensor(out=n[:, dst, :], in0=n[:, 4, :], scalar=1.5,
                                                         in1=n[:, src, :], op0=ALU.add, op1=ALU.mult)
                    if dst < 7:
                        chained(end, 5 + 3 * q)
                end.then_inc(rstd_made[k], 1)
                chain_over()

            def norm(g, k, dst):
                dve.wait_ge(rstd_made[k], g + 1)
                for t in range(G):
                    end = nc.vector.tensor_scalar(dst[:, t, 0:D],
                                                  x_tile(g, t),
                                                  moments[:, k, t, 0:1], newton[:, k, 7, t:t + 1],
                                                  ALU.subtract, ALU.mult)
                return end

            def norm_x(g):
                norm(g, 0, xn).then_inc(xn_made, 1)

            def score_max(g):
                dve.wait_ge(scored, g + 1)
                chained(nc.vector.tensor_reduce(out=small[:, 0, :], in_=score_ps, axis=AX.X, op=ALU.max), 1)
                nc.vector.tensor_scalar(small[:, 1, :], small[:, 0, :], -(D ** -0.5), None, ALU.mult
                                        ).then_inc(max_made, 1)
                chain_over()

            def attend(g):
                dve.wait_ge(exp_made, g + 1)
                chained(nc.vector.reciprocal(small[:, 3, :], small[:, 2, :]), 1)
                chained(nc.vector.tensor_tensor(small[:, 4, :], small[:, 3, :], valid_gate[:, bass.ds(g * G, G)],
                                                ALU.mult), 2)
                chain_over()
                dve.wait_ge(readout_done, g + 1)
                for t in range(G):
                    xt = x_tile(g, t)
                    end = nc.vector.scalar_tensor_tensor(out=xt, in0=read_ps[:, t, :], scalar=small[:, 4, t:t + 1],
                                                         in1=xt, op0=ALU.mult, op1=ALU.add)
                chained(end, 1)

            def norm_x2(g):
                wait(dve, rows_stored, g * 16)
                norm(g, 1, rows).then_inc(x2n_made, 1)

            def low_x2n(g, h):
                dve.wait_ge(xTh_made, 2 * g + h + 1)
                view = [a.rearrange("p (c t n) -> p t c n", c=KC, t=G)[:, 2 * h:2 * h + 2, :, :]
                        for a in (xTl[:, :], xTh[:, :].bitcast(f32))]
                for t in range(2):
                    end = nc.vector.tensor_tensor(view[0][:, t, :, :], x2T_ps[h][:, t, :, :], view[1][:, t, :, :],
                                                  ALU.subtract)
                end.then_inc(xTl_made, 1)

            def route(g):
                dve.wait_ge(logits_done, g + 1)
                chained(nc.vector.tensor_copy(router[:, 0, :, :], logit_ps[:, :, 1, :]), 1)
                chained(nc.vector.tensor_tensor(router[:, 2, :, :], logit_ps[:, :, 0, :], router[:, 0, :, :], ALU.add), 2)
                chained(nc.vector.tensor_reduce(out=rsmall[:, 0, :], in_=router[:, 2, :, :], axis=AX.X, op=ALU.max), 3)
                nc.vector.tensor_tensor(router[:, 1, :, :], router[:, 2, :, :],
                                        rsmall[:, 0, :].unsqueeze(2).to_broadcast([P, G, E]), ALU.subtract
                                        ).then_inc(logits_shifted, 1)
                dve.wait_ge(route_exp, g + 1)
                chained(nc.vector.tensor_reduce(out=rsmall[:, 1, :], in_=router[:, 0, :, :], axis=AX.X, op=ALU.add), 4)
                chained(nc.vector.reciprocal(rsmall[:, 2, :], rsmall[:, 1, :]), 5)
                chained(nc.vector.tensor_tensor(router[:, 1, :, :], router[:, 0, :, :],
                                                rsmall[:, 2, :].unsqueeze(2).to_broadcast([P, G, E]), ALU.mult), 6)
                for t in range(G):
                    end = nc.vector.max(out=top8[:, t, :], in_=router[:, 1, t, :])
                chained(end, 7)
                chained(nc.vector.memset(top8[:, :, TOPK:8], -1.0), 8)
                for t in range(G):
                    end = nc.vector.match_replace(out=router[:, 2, t, :], in_to_replace=top8[:, t, :],
                                                  in_values=router[:, 1, t, :], imm_value=-1.0)
                chained(end, 9)
                now = chosen[:, bass.ds(g * G, G), :]
                chained(nc.vector.tensor_scalar(now, router[:, 2, :, :], 0.0, None, ALU.is_lt), 10)
                nc.vector.scalar_tensor_tensor(out=rows[:, :, D:ROW], in0=router[:, 1, :, :], scalar=half_tanh[:, :],
                                               in1=now, op0=ALU.mult, op1=ALU.mult).then_inc(weights_made, 1)
                chain_over()

            def shared_act(g, c):
                r = srows(c)
                a = act_s[0:r, c % 2, :]
                dve.wait_ge(s_tanh_made, 3 * g + c + 1)
                chained(nc.vector.scalar_tensor_tensor(out=a, in0=a, scalar=1.0, in1=gate_ps[c % 2][0:r, :],
                                                       op0=ALU.add, op1=ALU.mult), 1)
                nc.vector.scalar_tensor_tensor(out=a, in0=a, scalar=half_tanh[0:r, :], in1=up_ps[c % 2][0:r, :],
                                               op0=ALU.mult, op1=ALU.mult).then_inc(s_act_made, 1)
                chain_over()

            def one_hots(t):
                if t >= HOT:
                    dve.wait_ge(hot_used, t - HOT + 1)
                for of, number, width in ((hot_slot, slot_no, P), (hot_tile01, tile_no, ST)):
                    end = nc.vector.tensor_tensor(of[:, t % HOT, :, :], iotas[:, 0:width, :],
                                                  number[:, t, 0:TOPK].unsqueeze(1).to_broadcast([P, width, TOPK]),
                                                  ALU.is_equal)
                end.then_inc(hot_made, 1)

            dve.wait_ge(x_arrived, 16)
            moments_of(0, 0)
            rstd_here(0, 0)
            norm_x(0)
            dve.wait_ge(consts_in, 16 * 5)
            nc.vector.tensor_reduce(out=any_valid[:, :], in_=mask_in, axis=AX.X, op=ALU.max).then_inc(valid_reduced, 1)
            nc.vector.memset(zero[:, :], 0.0).then_inc(zero_made, 1)
            nc.vector.tensor_scalar(bias[:, :, :], mask_in, 1.0, -MASKED, ALU.subtract, ALU.mult
                                    ).then_inc(bias_made, 1)
            dve.wait_ge(gate_parts, 1)
            nc.vector.tensor_tensor(Gl, raw_gate[:, :, :], Gh.bitcast(f32), ALU.subtract
                                    ).then_inc(gate_parts, 1)
            dve.wait_ge(gates_made, 1)
            nc.vector.tensor_scalar(half_tanh[:, :], gate_tanh[:, 1:2], 0.5, None, ALU.mult)
            dve.wait_ge(valid_spread, 1)
            nc.vector.tensor_scalar(valid_gate[:, :], valid_ps, gate_tanh[:, 0:1], None, ALU.mult
                                    ).then_inc(valid_made, 1)
            dve.wait_ge(x_arrived, 32)
            moments_of(0, 1)
            score_max(0)
            nc.vector.tensor_copy(iotas[:, :, :],
                                  const[:, C_IOTA:C_IOTA + P].unsqueeze(2).to_broadcast([P, P, TOPK]))
            nc.vector.tensor_copy(tri[:, :], const[:, C_TRI:C_TRI + P])
            nc.vector.memset(ones[:, :], 1.0)
            nc.vector.memset(prefix[:, :, :], 0.0)
            nc.vector.memset(zeros16[:, :], 0.0).then_inc(routing_consts, 1)
            norm_x(1)
            attend(0)
            moments_of(1, 0)
            rstd_here(0, 1)
            norm_x2(0)

            def body(n, front=True):
                shared_act(n, 0)
                route(n)
                score_max(n + 1)
                if front:
                    dve.wait_ge(x_arrived, n * 16 + 48)
                shared_low(n, 0)
                if front:
                    moments_of(0, n + 2)
                shared_act(n, 1)
                attend(n + 1)
                moments_of(1, n + 1)
                rstd_here(n + 1, 1)
                norm_x2(n + 1)
                shared_low(n, 1)
                shared_act(n, 2)
                if front:
                    norm_x(n + 2)
                shared_low(n, 2)
                low_x2n(n + 1, 0)
                low_x2n(n + 1, 1)

            low_x2n(0, 0)
            low_x2n(0, 1)
            groups(dve, body)
            n = NGRP - 1
            shared_act(n, 0)
            route(n)
            shared_low(n, 0)

            dve.wait_ge(ranked, 1)
            over = wide[:, 0, :].rearrange("p (e k) -> p e k", e=E)
            chained(nc.vector.tensor_tensor(over, rank_ps[:, T, :].unsqueeze(2).to_broadcast([P, E, T]),
                                            const[:, C_K128:C_K128 + T].unsqueeze(1).to_broadcast([P, E, T]),
                                            ALU.is_gt), 1)
            chained(nc.vector.tensor_reduce(out=tiles_of[:, :], in_=over, axis=AX.X, op=ALU.add), 2)
            chained(nc.vector.tensor_copy(prefix[:, 0, 8:], tiles_of[:, :]), 3)
            for q in range(4):
                d = 1 << q
                chained(nc.vector.tensor_tensor(prefix[:, (q + 1) % 2, 8:], prefix[:, q % 2, 8:],
                                                prefix[:, q % 2, 8 - d:8 + E - d], ALU.add), 4 + q)
            chained(nc.vector.tensor_scalar(prefix[:, 1, 8:], prefix[:, 0, 8:], const[:, C_ID1:C_ID1 + 1], None,
                                            ALU.is_lt), 8)
            chained(nc.vector.tensor_reduce(out=expert_of[:, 0:1], in_=prefix[:, 1, 8:], axis=AX.X, op=ALU.add), 9)
            nc.vector.tensor_scalar(expert_of[:, 1:2], expert_of[:, 0:1], float(E - 1), None, ALU.min
                                    ).then_inc(expert_counted, 1)
            chained(nc.vector.tensor_tensor(base[:, 0, :], prefix[:, 0, 8:], tiles_of[:, :], ALU.subtract), 10)
            chained(nc.vector.tensor_scalar(base[:, 1, :], base[:, 0, :], float(P), 1.0, ALU.mult, ALU.add), 11)
            w0, w1_ = (wide[:, q, :].rearrange("p (t e) -> p t e", e=E) for q in range(2))
            chained(nc.vector.tensor_tensor(w0, rank_ps[:, 0:T, :],
                                            base[:, 1, :].unsqueeze(1).to_broadcast([P, T, E]), ALU.add), 12)
            chained(nc.vector.tensor_tensor(w1_, w0, chosen[:, :, :], ALU.mult), 13)
            for t in range(T):
                end = nc.vector.max(out=places[:, t, :], in_=w1_[:, t, :])
            chained(end, 14)
            flat = places[:, :, :].rearrange("p t k -> p (t k)")
            chained(nc.vector.tensor_scalar(place_bits[:, 0, :], flat, -1.0, None, ALU.add), 15)
            nc.vector.tensor_single_scalar(place_bits[:, 1, :], place_bits[:, 0, :], 7, op=ALU.arith_shift_right)
            chained(nc.vector.tensor_single_scalar(place_bits[:, 2, :], place_bits[:, 0, :], P - 1,
                                                   op=ALU.bitwise_and), 16)
            nc.vector.tensor_copy(tile_no[:, :, :].rearrange("p t k -> p (t k)"), place_bits[:, 1, :])
            nc.vector.tensor_copy(slot_no[:, :, :].rearrange("p t k -> p (t k)"), place_bits[:, 2, :]
                                  ).then_inc(places_made, 1)
            chain_over()
            for c in (1, 2):
                shared_act(n, c)
                shared_low(n, c)
            dve.wait_ge(places_made, 1)
            dve.wait_ge(low_made, 3 + E)
            for t in range(T):
                one_hots(t)
            dve.wait_ge(hot_used, T)
            chained(nc.vector.tensor_scalar(wide[:, 0, 0:ST], inverse_ps, 0.0, const[:, C_PAD:C_PAD + 1],
                                            ALU.is_equal, ALU.mult), 1)
            nc.vector.scalar_tensor_tensor(out=slot_ids[:, :], in0=inverse_ps, scalar=-1.0, in1=wide[:, 0, 0:ST],
                                           op0=ALU.add, op1=ALU.add).then_inc(ids_made, 1)
            chain_over()
            dve.wait_ge(ids_made, 1)
            dve.wait_ge(expert_made, 1)

            def step(j, k, i, experts):
                static = isinstance(j, int)

                def low_rows(j1, k1):
                    dve.wait_ge(c_xTh_made, j1 + 1)
                    at = slice((k1 % 2) * 2 * P, (k1 % 2 + 1) * 2 * P)
                    nc.vector.tensor_tensor(xTl[:, at], gT_ps[:, k1 % 2, 0:2 * P], xTh[:, at].bitcast(f32),
                                            ALU.subtract).then_inc(c_xTl_made, 1)

                def ids(ring, j1, k1, made):
                    nc.vector.tensor_copy(ring[:, k1:k1 + 1], slot_ids[:, bass.ds(j1, 1)]).then_inc(made, 1)

                if static and j == 0:
                    for q in range(AHEAD + 1):
                        ids(gather_ids, q, q, gather_ids_made)
                    low_rows(0, 0)
                if not static or j + 1 < ST:
                    low_rows(j + 1, k + 1)
                if not static or j < ST:
                    dve.wait_ge(c_tanh_made, j + 1)
                    e = experts[k]
                    g = gated[:, k % 2, :]
                    nc.vector.scalar_tensor_tensor(out=g, in0=g, scalar=1.0, in1=gu_ps[:, k % 2, 0:I],
                                                   op0=ALU.add, op1=ALU.mult).then_inc(c_gated_made, 1)
                    dve.wait_ge(c_gated_made, j + 1)
                    nc.vector.scalar_tensor_tensor(out=hidden[:, k % 2, :], in0=g, scalar=rows[:, k % R, bass.ds(e + D, 1)],
                                                   in1=gu_ps[:, k % 2, I:2 * I], op0=ALU.mult, op1=ALU.mult
                                                   ).then_inc(c_hidden_made, 1)
                if not static or j + R < ST:
                    ids(gather_ids, j + R, k % R, gather_ids_made)
                if (not static) or 2 <= j <= ST + 1:
                    wait(dve, scattered[(k - 2) % R], (i * (U // R) + (k - 2) // R) * 16)
                if (not static) or 1 <= j <= ST:
                    k1 = (k - 1) % 2
                    dve.wait_ge(c_hTh_made, j)
                    nc.vector.tensor_tensor(hTl[:, k1, :, :], hT_ps[0:IR, k1, 0:IC * P].rearrange("p (c n) -> p c n", c=IC),
                                            hTh[:, k1, :, :].bitcast(f32), ALU.subtract).then_inc(c_hTl_made, 1)
                if (not static) or 2 <= j <= ST + 1:
                    k2 = (k - 2) % R
                    ids(scatter_ids, j - 2, k2, scatter_ids_made)

            slot_tiles(dve, step, lambda i: turn_experts(dve, i, 0))

            for g in range(NGRP):
                dve.wait_ge(parts_in[g % 2], 32 * (g // 2 + 1))
                a, b = (part[:, g % 2, q, :, :].rearrange("p t d -> p (t d)") for q in range(2))
                nc.vector.tensor_tensor(a, a, b, ALU.add).then_inc(summed, 1)

        @block.gpsimd
        def _(pool):
            def rstd(g):
                n = newton[:, 0, :, :]
                step = [0]

                def chained(ins):
                    step[0] += 1
                    ins.then_inc(pool_step, 1)
                    pool.wait_ge(pool_step, step[0])

                pool.wait_ge(moments_made[0], g + 1)
                chained(nc.gpsimd.tensor_tensor(n[:, 0, :], moments[:, 0, :, 1], eps[:, :], ALU.add))
                nc.gpsimd.tensor_scalar(n[:, 1, :], n[:, 0, :], -0.5, None, ALU.mult)
                chained(nc.gpsimd.tensor_scalar(n[:, 2, :].bitcast(i32), n[:, 0, :].bitcast(i32), -0.5,
                                                float(0x5f3759df), ALU.mult, ALU.add))
                for src, dst in ((2, 5), (5, 6), (6, 7)):
                    chained(nc.gpsimd.tensor_tensor(n[:, 3, :], n[:, src, :], n[:, src, :], ALU.mult))
                    chained(nc.gpsimd.tensor_tensor(n[:, 4, :], n[:, 3, :], n[:, 1, :], ALU.mult))
                    chained(nc.gpsimd.tensor_scalar(n[:, 3, :], n[:, 4, :], 1.5, None, ALU.add))
                    end = nc.gpsimd.tensor_tensor(n[:, dst, :], n[:, 3, :], n[:, src, :], ALU.mult)
                    if dst < 7:
                        chained(end)
                end.then_inc(rstd_made[0], 1)
                pool.sem_clear(pool_step)

            def low(dst, k, high, cols, value):
                pool.wait_ge(high_made, value)
                nc.gpsimd.tensor_tensor(dst, raw[:, k, 0:cols], high, ALU.subtract).then_inc(low_made, 1)

            def low_expert(e, k, value):
                low(W1l[:, bass.ds(e, 1), :, :].rearrange("p e c n -> p (e c n)"), k,
                    W1h[:, bass.ds(e, 1), :, :].bitcast(f32).rearrange("p e c n -> p (e c n)"), W1C, value)

            nc.gpsimd.memset(eps[:, :], EPS).then_inc(pool_step, 1)
            pool.wait_ge(pool_step, 1)
            pool.sem_clear(pool_step)
            rstd(1)
            for k in range(2):
                low(W1sl[:, k, :], k, W1sh[:, k, :].bitcast(f32), 2 * SI, k + 1)
            low(W2sl[:, :, :].rearrange("p c n -> p (c n)"), 2, W2sh[:, :, :].bitcast(f32).rearrange("p c n -> p (c n)"),
                SC * D, 3)
            for k in range(4):
                low_expert(k, (3 + k) % 4, 4 + k)

            def body(n, front=True):
                def expert(k):
                    low_expert(n * 4 + 4 + k, (3 + k) % 4, n * 4 + 8 + k)

                if front:
                    rstd(n + 2)
                for k in range(4):
                    expert(k)

            groups(pool, body)

            for q in range(E // 2):
                pool.wait_ge(high2_made, q + 1)
                at = slice(2 * q, 2 * q + 2)
                nc.gpsimd.tensor_tensor(W2l[:, at, :, :].rearrange("p e c n -> p (e c n)"),
                                        raw2[:, q % 2, :, :].rearrange("p e n -> p (e n)"),
                                        W2h[:, at, :, :].bitcast(f32).rearrange("p e c n -> p (e c n)"),
                                        ALU.subtract).then_inc(low2_made, 1)

            def no_wait_in_dma():
                pool.sem_inc(dma_allowed, 1)

            def gather(j, k):
                pool.wait_ge(gather_ids_made, j + 1)
                no_wait_in_dma()
                nc.gpsimd.indirect_dma_start(
                    out=rows[:, k, :], out_offset=None, in_=rows_dram,
                    in_offset=bass.IndirectOffsetOnAxis(ap=gather_ids[:, k:k + 1], axis=0),
                    bounds_check=N + P - 1).then_inc(gathered[k], 16)

            def step(j, k, i, experts):
                static = isinstance(j, int)
                if static and j == 0:
                    for q in range(AHEAD):
                        gather(q, q)
                if not static or j + AHEAD < ST:
                    wait(pool, c_hidden_made, j)
                    gather(j + AHEAD, (k + AHEAD) % R)
                if not static or j >= 3:
                    k3 = (k - 3) % R
                    wait(pool, scattered[(k - 5) % R], (i * (U // R) + (k - 5) // R + 1) * 16)
                    pool.wait_ge(scatter_ids_made, j - 2)
                    pool.wait_ge(c_y_made, j - 2)
                    no_wait_in_dma()
                    nc.gpsimd.indirect_dma_start(
                        out=sums[k3 % 2], out_offset=bass.IndirectOffsetOnAxis(ap=scatter_ids[:, k3:k3 + 1], axis=0),
                        in_=y[:, k3, :], in_offset=None, bounds_check=N + P - 1,
                        compute_op=ALU.add).then_inc(scattered[k3], 16)

            pool.wait_ge(ids_made, 1)
            pool.wait_ge(pads_stored, 16 * 3)
            pool.wait_ge(rows_stored, 16 * NGRP)
            pool.wait_ge(x2_stored, 16 * NGRP)
            for h in range(2):
                pool.wait_ge(shared_stored[h], 16 * NGRP)
            slot_tiles(pool, step)


def kernel(x, ctx_2048, mask_BxS2_bk0, g_xattn, g_ffn, L0_ffn_gate_w, L0_ffn_w1, L0_ffn_w2,
           L0_ffn_shared_w1, L0_ffn_shared_w2):
    import numpy as np
    import concourse.bacc as bacc
    from concourse.bass_utils import run_bass_kernel_spmd

    c, f = np.ascontiguousarray, np.float32
    x, ctx = np.asarray(x).reshape(N, D), np.asarray(ctx_2048).reshape(N, D)
    ctx_t = c(ctx.reshape(T, P, KC, P).transpose(3, 0, 2, 1))
    mask = np.zeros((BT, T, P), np.uint8)
    bits = np.asarray(mask_BxS2_bk0).view(np.uint8).reshape(T, BT, M)
    for b in range(BT):
        mask[b, :, b * M:(b + 1) * M] = bits[:, b, :]
    mask = mask.view(np.int32)
    gates = c(np.broadcast_to(np.concatenate([np.asarray(g_xattn), np.asarray(g_ffn)])[None, :], (P, 2)))
    gate_w = c(np.asarray(L0_ffn_gate_w).T.reshape(KC, P, E).transpose(1, 0, 2))
    w1 = c(np.asarray(L0_ffn_w1).reshape(E, 2 * I, KC, P).transpose(0, 3, 2, 1).reshape(E, P, W1C))
    w1s = c(np.asarray(L0_ffn_shared_w1).reshape(2 * SI, KC, P).transpose(2, 1, 0))
    w2 = c(np.asarray(L0_ffn_w2).reshape(E, D, IC, IR).transpose(3, 0, 2, 1).reshape(IR, E, IC * D))
    w2s = np.concatenate([np.asarray(L0_ffn_shared_w2).T, np.zeros((SC * P - SI, D), f)])
    w2s = c(w2s.reshape(SC, P, D).transpose(1, 0, 2).reshape(P, SC * D))
    n = np.arange(P)
    consts = np.zeros((P, C_END), f)
    consts[:, C_IDENT:C_IDENT + P] = np.eye(P)
    consts[:, C_IOTA:C_IOTA + P] = n[None, :]
    consts[:, C_TRI:C_TRI + P] = n[:, None] < n[None, :]
    consts[:, C_K128:C_K128 + T] = P * np.arange(T)[None, :]
    consts[:, C_ID1:C_ID1 + T] = P * np.arange(T)[None, :] + n[:, None] + 1
    consts[:, C_PAD] = N + 1 + n
    sel = c(np.repeat(np.eye(BT, dtype=f), S, axis=1))

    arrays = {"x": x, "ctx_n": ctx, "ctx_t": ctx_t, "mask": mask, "gates": gates, "gate_w": gate_w,
              "w1": w1, "w1s": w1s, "w2": w2, "w2s": w2s, "consts": consts, "sel": sel}
    nc = bacc.Bacc("TRN2", target_bir_lowering=False, num_devices=1)
    args = {k: nc.dram_tensor("in_" + k, a.shape, mybir.dt.from_np(a.dtype), kind="ExternalInput").ap()
            for k, a in arrays.items()}
    out = nc.dram_tensor("out", (N, D), mybir.dt.float32, kind="ExternalOutput").ap()
    sparse_block(nc, out=out, **args)
    r = run_bass_kernel_spmd(nc, [{"in_" + k: c(a) for k, a in arrays.items()}], core_ids=[0])
    return r.results[0]["out"].reshape(B, S, D)
```

```python
from contextlib import ExitStack

import concourse.bass as bass
from concourse import mybir

B, S, M, D = 32, 64, 64, 256
P = 128
N = B * S
T = N // P
BT = P // S
KC = D // P
G = 4
NGRP = T // G
GT = G * P
E, I, TOPK = 16, 176, 6
IC = 2
IR = I // IC
SI = 352
SC = -(-SI // P)
W1C = KC * 2 * I
ROW = D + E
U = 8
R = 4
ST = (TOPK * N + E * (P - 1)) // P
SW = -(-ST // U) * U
EPS = 1e-5
MASKED = -1e30 * D ** 0.5
AHEAD = 3

C_IDENT, C_IOTA, C_TRI, C_K128, C_ID1, C_PAD, C_END = 0, 128, 256, 384, 400, 416, 417
RAW2 = 3
LATE2 = 7
BY_POOL2 = (0, 1, 2, 3, 4)
HOT = 4


def srows(c):
    return min(P, SI - c * P)


def sparse_block(nc, x, ctx_n, ctx_t, mask, gates, gate_w, w1, w1s, w2, w2s, consts, sel, out):
    f32, f32r, f16 = mybir.dt.float32, mybir.dt.float32r, mybir.dt.float16
    u8, i32, u32 = mybir.dt.uint8, mybir.dt.int32, mybir.dt.uint32
    ALU, ACT, AX = mybir.AluOpType, mybir.ActivationFunctionType, mybir.AxisListType

    rows_dram = nc.dram_tensor("rows_dram", (N + P, ROW), f32, kind="Internal").ap()
    sums = [nc.dram_tensor(f"sum_{k}", (N + P, D), f32, kind="Internal").ap() for k in "xy"]

    with ExitStack() as stack:
        def sem(name):
            return stack.enter_context(nc.semaphore(name))

        def allocator(s):
            return lambda name, shape, dt=f32: s.enter_context(nc.sbuf_tensor(name, shape, dt))

        sb = allocator(stack)
        W1h, W1l = sb("W1h", [P, E, KC, 2 * I], f32r), sb("W1l", [P, E, KC, 2 * I], f32r)
        const = sb("const", [P, C_END])
        gates_in, gate_tanh, half_tanh = sb("gates_in", [P, 2]), sb("gate_tanh", [P, 2]), sb("half_tanh", [P, 1])
        rows = sb("rows", [P, G, ROW])
        xTh, xTl = sb("xTh", [P, KC * GT], f32r), sb("xTl", [P, KC * GT], f32r)
        y = sb("y", [P, G, D])
        chosen = sb("chosen", [P, T, E], f16)
        slot_ids = sb("slot_ids", [P, SW], u32)
        tile_expert = sb("tile_expert", [1, SW], i32)
        gather_ids, scatter_ids = sb("gather_ids", [P, R], u32), sb("scatter_ids", [P, R], u32)
        iotas, tri = sb("iotas", [P, P, TOPK], f16), sb("tri", [P, P], f16)
        ones, zeros16 = sb("ones", [P, P], f16), sb("zeros16", [P, (T + 1) * E], f16)
        tiles_of, expert_of = sb("tiles_of", [P, E]), sb("expert_of", [P, 2])
        prefix = sb("prefix", [P, 2, 8 + E])
        wide = sb("wide", [P, 2, T * E])
        base = sb("base", [P, 2, E])
        places = sb("places", [P, T, 8])
        place_bits = sb("place_bits", [P, 3, T * 8], i32)
        tile_no, slot_no = sb("tile_no", [P, T, 8], f16), sb("slot_no", [P, T, 8], f16)

        first = ExitStack()
        sb = allocator(first)
        RAWC = max(W1C, SC * D)
        raw = sb("raw", [P, 4, RAWC])
        probs, probsT = sb("probs", [P, G, P]), sb("probsT", [P, G, P])
        ctx_in, ctxT_in = sb("ctx_in", [P, G, D]), sb("ctxT_in", [P, G, KC, P])
        xn, xnT = sb("xn", [P, G, D]), sb("xnT", [P, G, KC, P])
        mask_words = sb("mask_words", [BT, T, P // 4], i32)
        mask_in = mask_words[:, :, :].bitcast(u8)
        bias, selector_r = sb("bias", [BT, T, P], f32r), sb("selector_r", [BT, P], f32r)
        x_in = sb("x_in", [P, 2, G, D])
        W1sh, W1sl = sb("W1sh", [P, KC, 2 * SI], f32r), sb("W1sl", [P, KC, 2 * SI], f32r)
        gate_parts_r = sb("gate_parts_r", [P, KC, 2, E], f32r)
        Gh, Gl = gate_parts_r[:, :, 0, :], gate_parts_r[:, :, 1, :]
        raw_gate = sb("raw_gate", [P, KC, E])
        any_valid, selector = sb("any_valid", [BT, T]), sb("selector", [BT, P])
        valid_gate = sb("valid_gate", [P, T])
        stats, moments = sb("stats", [P, 2, G, 6]), sb("moments", [P, 2, G, 2])
        newton, eps = sb("newton", [P, 2, 8, G]), sb("eps", [P, G])
        shift, shift2 = sb("shift", [P, G]), sb("shift2", [P, G])
        small = sb("small", [P, 8, G])
        router = sb("router", [P, 3, G, E])
        rsmall = sb("rsmall", [P, 4, G])
        top8 = sb("top8", [P, G, 8])
        W2sh, W2sl = sb("W2sh", [P, SC, D], f32r), sb("W2sl", [P, SC, D], f32r)
        act_s = sb("act_s", [P, 2, GT])
        hsh, hsl = sb("hsh", [P, SC, GT], f32r), sb("hsl", [P, SC, GT], f32r)
        zero = sb("zero", [P, ROW])
        first.close()

        HOT_BYTES = 2 * HOT * TOPK * (P + 2 * SW)
        hot = ExitStack()
        sb = allocator(hot)
        hot_slot = sb("hot_slot", [P, HOT, P, TOPK], f16)
        hot_tile01 = sb("hot_tile01", [P, HOT, SW, TOPK], f16)
        hot_tile = sb("hot_tile", [P, HOT, SW, TOPK], f16)
        hot.close()

        later = ExitStack()
        sb = allocator(later)
        gated, hidden = sb("gated", [P, 2, I]), sb("hidden", [P, 2, I])
        hTh, hTl = sb("hTh", [IR, 2, IC, P], f32r), sb("hTl", [IR, 2, IC, P], f32r)
        sb("hot_rest", [P, HOT_BYTES // 4 - 4 * I - 4 * IC * P])
        raw2 = sb("raw2", [IR, RAW2, 2, IC * D])
        W2 = sb("W2", [IR, E, 2, IC * D], f32r)
        W2h, W2l = W2[:, :, 0, :], W2[:, :, 1, :]
        later.close()

        last = ExitStack()
        sb = allocator(last)
        part = sb("part", [P, NGRP, 2, G, D])
        last.close()

        bank = stack.enter_context(nc.psum_tensor("bank", [P, 8, 512], f32))
        xnT_ps = bank[:, 0:2, :].rearrange("p b (t c n) -> p (b t) c n", t=2, c=KC)
        read_ps = bank[:, 0:2, :].rearrange("p b (t n) -> p (b t) n", t=2)
        score_ps = bank[:, 2, :].rearrange("p (t n) -> p t n", t=G)
        x2T_ps = [bank[:, b, :].rearrange("p (t c n) -> p t c n", t=2, c=KC) for b in (0, 1)]
        logit_ps, last_logit_ps = (bank[:, b, 0:G * 2 * E].rearrange("p (t q e) -> p t q e", t=G, q=2) for b in (3, 2))
        outs_ps = [bank[:, 3, :].rearrange("p (t n) -> p t n", t=2), bank[:, 6:8, 0:D]]
        gate_ps, up_ps = [bank[:, 4, :], bank[:, 6, :]], [bank[:, 5, :], bank[:, 7, :]]
        valid_ps = bank[:, 7, 0:T]
        rank_ps = bank[:, 0, 0:(T + 1) * E].rearrange("p (t e) -> p t e", e=E)
        inverse_ps = bank[:, 1, 0:SW]
        expert_ps = bank[0:1, 2, 0:P]
        gT_ps, gu_ps, hT_ps, y_ps = bank[:, 0:2, :], bank[:, 2:4, :], bank[:, 4:6, :], bank[:, 6:8, :]

        consts_in, x_arrived, ctx_arrived = sem("consts_in"), sem("x_arrived"), sem("ctx_arrived")
        raw_in = [sem(f"raw_in_{k}") for k in range(4)]
        raw2_in = [sem(f"raw2_in_{k}") for k in range(RAW2)]
        x2_stored, rows_stored, weights_stored, pads_stored = (
            sem("x2_stored"), sem("rows_stored"), sem("weights_stored"), sem("pads_stored"))
        shared_stored = [sem("shared_stored_0"), sem("shared_stored_1")]
        gates_made, valid_reduced, valid_spread, valid_made, bias_made, routing_consts, zero_made, gate_parts = (
            sem("gates_made"), sem("valid_reduced"), sem("valid_spread"), sem("valid_made"), sem("bias_made"),
            sem("routing_consts"), sem("zero_made"), sem("gate_parts"))
        high_made, low_made = sem("high_made"), sem("low_made")
        gather_ids_made, scatter_ids_made = sem("gather_ids_made"), sem("scatter_ids_made")
        x_seen, dma_allowed = sem("x_seen"), sem("dma_allowed")
        high2_made, low2_made = sem("high2_made"), [sem("low2_by_vector"), sem("low2_by_pool")]
        moments_made = [sem("moments_made"), sem("moments2_made")]
        rstd_made = [sem("rstd_made"), sem("rstd2_made")]
        shift_made = sem("shift_made")
        xn_made, xnT_done, xnT_made = sem("xn_made"), sem("xnT_done"), sem("xnT_made")
        scored, max_made, exp_made = sem("scored"), sem("max_made"), sem("exp_made")
        probsT_done, probsT_made, readout_done = sem("probsT_done"), sem("probsT_made"), sem("readout_done")
        shift2_made = sem("shift2_made")
        x2n_made = [sem("x2n_made"), sem("x2n_rest_made")]
        x2T_done, xTh_made, xTl_made = sem("x2T_done"), sem("xTh_made"), sem("xTl_made")
        logits_done, logits_shifted, route_exp, weights_made = (
            sem("logits_done"), sem("logits_shifted"), sem("route_exp"), sem("weights_made"))
        s_up_done, s_tanh_made, s_act_made, s_high_made, s_low_made, s_last_low_made = (
            sem("s_up_done"), sem("s_tanh_made"), sem("s_act_made"), sem("s_high_made"), sem("s_low_made"),
            sem("s_last_low_made"))
        s_down_done, s_out_made = sem("s_down_done"), sem("s_out_made")
        ranked, places_made = sem("ranked"), sem("places_made")
        hot_made, hot_scaled, hot_used = (
            sem("hot_made"), sem("hot_scaled"), sem("hot_used"))
        ids_made, expert_counted, expert_turned, expert_made = (
            sem("ids_made"), sem("expert_counted"), sem("expert_turned"), sem("expert_made"))
        vector_step, pool_step = sem("vector_step"), sem("pool_step")
        gathered = [sem(f"gathered_{k}") for k in range(R)]
        scattered = [sem(f"scattered_{k}") for k in range(R)]
        c_xT_done, c_xTh_made, c_xTl_made = sem("c_xT_done"), sem("c_xTh_made"), sem("c_xTl_made")
        c_up_done, c_tanh_made, c_gated_made, c_hidden_made = (
            sem("c_up_done"), sem("c_tanh_made"), sem("c_gated_made"), sem("c_hidden_made"))
        c_hT_done, c_hTh_made, c_hTl_made, c_down_done, c_y_made = (
            sem("c_hT_done"), sem("c_hTh_made"), sem("c_hTl_made"), sem("c_down_done"), sem("c_y_made"))
        parts_in = [sem(f"parts_in_{g}") for g in range(NGRP)]
        summed, out_stored = sem("summed"), sem("out_stored")

        block = stack.enter_context(nc.Block())
        identity = const[:, C_IDENT:C_IDENT + P]

        def wait(eng, s, value):
            if not (isinstance(value, int) and value <= 0):
                eng.wait_ge(s, value)

        def groups(eng, body):
            body(0)
            with eng.Fori(1, NGRP - 2) as n:
                body(n)
            body(NGRP - 2, front=False)

        def slot_tiles(eng, step, turn=None):
            turn = turn or (lambda i: None)
            experts = turn(0)
            for k in range(U):
                step(k, k, 0, experts)
            last = ST // U
            with eng.Fori(1, last) as i:
                experts = turn(i)
                for k in range(U):
                    step(i * U + k, k, i, experts)
            experts = turn(last)
            for k in range(ST - last * U + AHEAD):
                step(last * U + k, k, last, experts)

        turns_made = [0]

        def turn_experts(eng, i, before):
            turns_made[0] += 1
            regs = [eng.alloc_register(f"expert_{turns_made[0]}_{q}") for q in range(before + U)]
            eng.load(regs, tile_expert[0:1, bass.ds(i * U - before, len(regs))])
            return {q - before: bass.RuntimeValue.of_register_unchecked(reg, min_val=0, max_val=E - 1)
                    for q, reg in enumerate(regs)}

        def x_tile(g, t):
            return x_in[:, bass.ds(g % 2, 1), t, :].rearrange("p g d -> p (g d)")

        def high2(act, q):
            act.wait_ge(raw2_in[q % RAW2], 16 * (q // RAW2 + 1))
            nc.scalar.copy(W2h[:, 2 * q:2 * q + 2, :], raw2[:, q % RAW2, :, :]).then_inc(high2_made, 1)

        def low2(eng, engine, q):
            eng.wait_ge(high2_made, q + 1)
            at = slice(2 * q, 2 * q + 2)
            engine.tensor_tensor(W2l[:, at, :], raw2[:, q % RAW2, :, :], W2h[:, at, :].bitcast(f32), ALU.subtract
                                 ).then_inc(low2_made[q in BY_POOL2], 1)

        def shared_low(eng, engine, g, c):
            eng.wait_ge(s_high_made, 3 * g + c + 1)
            r = srows(c)
            engine.tensor_tensor(hsl[0:r, c, :], act_s[0:r, c % 2, :], hsh[0:r, c, :].bitcast(f32), ALU.subtract
                                 ).then_inc(s_low_made if c < 2 else s_last_low_made, 1)

        @block.sync
        def _(sp):
            def load_x(g):
                wait(sp, moments_made[0], g)
                wait(sp, x2_stored, (g - 1) * 16)
                wait(sp, x2n_made[0], g - 1)
                wait(sp, x2n_made[1], g - 1)
                sp.dma_start(x_in[:, g % 2, :, :],
                             x[bass.ds(g * GT, GT), :].rearrange("(t p) d -> p t d", p=P)).then_inc(x_arrived, 16)

            def load_ctx(g):
                wait(sp, readout_done, g)
                sp.dma_start(ctxT_in[:, :, :, :], ctx_t[:, bass.ds(g * G, G), :, :]).then_inc(ctx_arrived, 16)
                sp.dma_start(ctx_in[:, :, :], ctx_n[bass.ds(g * GT, GT), :].rearrange("(t p) d -> p t d", p=P)
                             ).then_inc(ctx_arrived, 16)

            def load_piece(k, src, cols, made):
                wait(sp, low_made, made)
                sp.dma_start(raw[:, k, 0:cols], src).then_inc(raw_in[k], 16)

            def store_x2(g):
                sp.wait_ge(moments_made[1], g + 1)
                sp.dma_start(sums[0][bass.ds(g * GT, GT), :].rearrange("(t p) d -> p t d", p=P),
                             x_in[:, g % 2, :, :]).then_inc(x2_stored, 16)

            def store_x2n(g):
                sp.wait_ge(x2n_made[0], g + 1)
                sp.wait_ge(x2n_made[1], g + 1)
                sp.dma_start(rows_dram[bass.ds(g * GT, GT), 0:D].rearrange("(t p) d -> p t d", p=P),
                             rows[:, :, 0:D]).then_inc(rows_stored, 16)

            def store_weights(g):
                sp.wait_ge(weights_made, g + 1)
                sp.dma_start(rows_dram[bass.ds(g * GT, GT), D:ROW].rearrange("(t p) d -> p t d", p=P),
                             rows[:, :, D:ROW]).then_inc(weights_stored, 16)

            def store_shared(g, h):
                sp.wait_ge(s_out_made, 2 * g + h + 1)
                sp.dma_start(sums[1][bass.ds(g * GT + h * 2 * P, 2 * P), :].rearrange("(t p) d -> p t d", p=P),
                             y[:, 2 * h:2 * h + 2, :]).then_inc(shared_stored[h], 16)

            def second_weights(pieces):
                sp.wait_ge(moments_made[1], NGRP)
                for q in pieces:
                    if q >= RAW2:
                        before = q - RAW2
                        pool = before in BY_POOL2
                        sp.wait_ge(low2_made[pool], sum((p in BY_POOL2) == pool for p in range(before + 1)))
                    sp.dma_start(raw2[:, q % RAW2, :, :], w2[:, 2 * q:2 * q + 2, :]).then_inc(raw2_in[q % RAW2], 16)

            load_x(0)
            for dst, src in ((const[:, :], consts), (mask_words[:, :, :], mask), (selector[:, :], sel),
                             (gates_in[:, :], gates), (raw_gate[:, :, :], gate_w)):
                sp.dma_start(dst, src).then_inc(consts_in, 16)
            load_ctx(0)
            load_x(1)
            load_piece(0, w1s[:, 0, :], 2 * SI, 0)
            load_piece(1, w1s[:, 1, :], 2 * SI, 0)
            load_piece(2, w2s[:, :], SC * D, 0)
            for k in range(3):
                load_piece((3 + k) % 4, w1[k, :, :], W1C, k)
            sp.wait_ge(zero_made, 1)
            sp.dma_start(rows_dram[N:N + P, :], zero[:, :]).then_inc(pads_stored, 16)
            for total in sums:
                sp.dma_start(total[N:N + P, :], zero[:, 0:D]).then_inc(pads_stored, 16)
            load_ctx(1)
            store_x2(0)
            store_x2n(0)
            load_x(2)
            load_piece(2, w1[3, :, :], W1C, 3)

            def body(n):
                for k in range(4):
                    sp.wait_ge(low_made, n * 4 + 4 + k)
                    sp.dma_start(raw[:, (3 + k) % 4, 0:W1C], w1[n * 4 + 4 + k, :, :]).then_inc(raw_in[(3 + k) % 4], 16)
                    if k == 1 and n + 2 < NGRP:
                        load_ctx(n + 2)
                store_x2(n + 1)
                store_x2n(n + 1)
                if n + 3 < NGRP:
                    load_x(n + 3)
                if n + 2 == NGRP:
                    second_weights(range(RAW2))
                store_weights(n)
                store_shared(n, 0)
                store_shared(n, 1)

            for n in range(NGRP - 1):
                body(n)
            store_weights(NGRP - 1)
            second_weights(range(RAW2, RAW2 + 2))
            store_shared(NGRP - 1, 0)
            store_shared(NGRP - 1, 1)
            second_weights(range(RAW2 + 2, E // 2))
            for k in range(R):
                sp.wait_ge(scattered[k], 16 * len(range(k, ST, R)))
            for g in range(NGRP):
                for a in range(2):
                    sp.dma_start(part[:, g, a, :, :],
                                 sums[a][g * GT:(g + 1) * GT, :].rearrange("(t p) d -> p t d", p=P)
                                 ).then_inc(parts_in[g], 16)
            for g in range(NGRP):
                sp.wait_ge(summed, g + 1)
                sp.dma_start(out[g * GT:(g + 1) * GT, :].rearrange("(t p) d -> p t d", p=P),
                             part[:, g, 0, :, :]).then_inc(out_stored, 16)
            sp.wait_ge(out_stored, 16 * NGRP)

        @block.tensor
        def _(pe):
            def split_product(dst, lh, ll, rh, rl, start, stop):
                nc.tensor.matmul(dst, lh, rh, start=start, stop=False)
                nc.tensor.matmul(dst, lh, rl, start=False, stop=False)
                return nc.tensor.matmul(dst, ll, rh, start=False, stop=stop)

            def transpose_xn(g):
                pe.wait_ge(xn_made, g + 1)
                wait(pe, moments_made[1], g)
                for t in range(G):
                    for c in range(KC):
                        end = nc.tensor.transpose(xnT_ps[:, t, c, :], xn[:, t, c * P:(c + 1) * P], identity)
                end.then_inc(xnT_done, 1)

            def scores(g):
                pe.wait_ge(ctx_arrived, g * 32 + 32)
                pe.wait_ge(xnT_made, g + 1)
                for t in range(G):
                    nc.tensor.matmul(score_ps[:, t, :], selector_r[:, :],
                                     bias[:, bass.ds(g * G + t, 1), :].rearrange("b t m -> b (t m)"),
                                     start=True, stop=False)
                    for c in range(KC):
                        end = nc.tensor.matmul(score_ps[:, t, :], xnT[:, t, c, :], ctxT_in[:, t, c, :],
                                               start=False, stop=c == KC - 1)
                end.then_inc(scored, 1)

            def transpose_probs(g):
                pe.wait_ge(exp_made, g + 1)
                for t in range(G):
                    end = nc.tensor.transpose(score_ps[:, t, :], probs[:, t, :], identity)
                end.then_inc(probsT_done, 1)

            def readout(g):
                pe.wait_ge(probsT_made, g + 1)
                for t in range(G):
                    end = nc.tensor.matmul(read_ps[:, t, :], probsT[:, t, :], ctx_in[:, t, :], start=True, stop=True)
                end.then_inc(readout_done, 1)

            def transpose_x2n(g, h):
                pe.wait_ge(xnT_made, min(g + 2, NGRP) if isinstance(g, int) else g + 2)
                pe.wait_ge(x2n_made[h], g + 1)
                for t in range(2):
                    for c in range(KC):
                        end = nc.tensor.transpose(x2T_ps[h][:, t, c, :], rows[:, 2 * h + t, c * P:(c + 1) * P], identity)
                end.then_inc(x2T_done, 1)

            def logits(g, into=logit_ps):
                pe.wait_ge(xTl_made, 2 * g + 2)
                if into is logit_ps:
                    wait(pe, s_out_made, 2 * g - 1)
                for t in range(G):
                    for n, (a, c) in enumerate((a, c) for a in (xTh, xTl) for c in range(KC)):
                        end = nc.tensor.matmul(into[:, t, :, :], a[:, c * GT + t * P:c * GT + (t + 1) * P],
                                               gate_parts_r[:, c, :, :], start=n == 0, stop=n == 2 * KC - 1)
                end.then_inc(logits_done, 1)

            def shared_up(g, c, parts=(0, 1)):
                pe.wait_ge(xTl_made, 2 * g + 2)
                if c == 1:
                    wait(pe, s_out_made, 2 * g)
                wait(pe, s_act_made, 3 * g + c - 1)
                r = srows(c)
                for dst, at in [((gate_ps[c % 2], 0), (up_ps[c % 2], SI))[q] for q in parts]:
                    for k in range(KC):
                        a = slice(at + c * P, at + c * P + r)
                        tok = slice(k * GT, (k + 1) * GT)
                        end = split_product(dst[0:r, :], W1sh[:, k, a], W1sl[:, k, a], xTh[:, tok], xTl[:, tok],
                                            k == 0, k == KC - 1)
                if 1 in parts:
                    end.then_inc(s_up_done, 1)

            def shared_down(g, h, c):
                if c < 2:
                    pe.wait_ge(s_low_made, 2 * g + c + 1)
                else:
                    pe.wait_ge(s_last_low_made, g + 1)
                if c == 0 and h == 0:
                    pe.wait_ge(route_exp, g + 1)
                if c == 0 and h == 1:
                    pe.wait_ge(s_act_made, 3 * g + 2)
                pieces = [(t, c) for t in ((0, 1) if h else (0,))]
                if h == 0 and c == SC - 1:
                    pieces += [(1, c1) for c1 in range(SC)]
                for t, c1 in pieces:
                    r, tok = srows(c1), slice((2 * h + t) * P, (2 * h + t + 1) * P)
                    end = split_product(outs_ps[h][:, t, :], hsh[0:r, c1, tok], hsl[0:r, c1, tok],
                                        W2sh[0:r, c1, :], W2sl[0:r, c1, :], c1 == 0, c1 == SC - 1)
                if c == SC - 1:
                    end.then_inc(s_down_done, 1)

            pe.wait_ge(consts_in, 16 * 5)
            transpose_xn(0)
            pe.wait_ge(bias_made, 1)
            pe.wait_ge(gate_parts, 2)
            scores(0)
            pe.wait_ge(valid_reduced, 1)
            nc.tensor.matmul(valid_ps, selector[:, :], any_valid[:, :], start=True, stop=True).then_inc(valid_spread, 1)
            transpose_probs(0)
            readout(0)
            transpose_xn(1)
            pe.wait_ge(valid_made, 1)
            def rank():
                pe.wait_ge(routing_consts, 1)
                pe.wait_ge(weights_made, NGRP)
                nc.tensor.matmul(bank[:, 0, 0:(T + 1) * E], ones[:, :], zeros16[:, :], start=True, stop=False)
                nc.tensor.matmul(bank[:, 0, 0:T * E], tri[:, :], chosen[:, :, :].rearrange("p t e -> p (t e)"),
                                 start=False, stop=False)
                for t in range(T):
                    later_tiles = chosen[:, t:t + 1, :].to_broadcast([P, T - t, E])
                    end = nc.tensor.matmul(rank_ps[:, t + 1:T + 1, :], ones[:, :], later_tiles,
                                           start=False, stop=t == T - 1)
                end.then_inc(ranked, 1)

            def body(n, front=True):
                logits(n)
                shared_up(n, 0, (0,))
                transpose_probs(n + 1)
                shared_up(n, 0, (1,))
                readout(n + 1)
                shared_up(n, 1)
                shared_up(n, 2)
                if front:
                    transpose_xn(n + 2)
                shared_down(n, 0, 0)
                transpose_x2n(n + 1, 0)
                transpose_x2n(n + 1, 1)
                if front:
                    scores(n + 2)
                    shared_down(n, 1, 0)
                else:
                    shared_down(n, 1, 0)
                    logits(NGRP - 1, last_logit_ps)
                shared_down(n, 0, 1)
                shared_down(n, 1, 1)
                shared_down(n, 0, 2)
                if not front:
                    rank()
                shared_down(n, 1, 2)

            transpose_x2n(0, 0)
            transpose_x2n(0, 1)
            pe.wait_ge(bias_made, 2)
            scores(1)
            pe.wait_ge(low_made, 3)
            groups(pe, body)
            n = NGRP - 1

            def use_hot(t):
                if t % 2:
                    pe.wait_ge(hot_made, t + 1)
                else:
                    pe.wait_ge(hot_scaled, t // 2 + 1)
                for r in range(TOPK):
                    end = nc.tensor.matmul(inverse_ps, hot_slot[:, t % HOT, :, r], hot_tile[:, t % HOT, :, r],
                                           start=t == 0 and r == 0, stop=t == T - 1 and r == TOPK - 1)
                end.then_inc(hot_used, 1)

            shared_up(n, 0)
            shared_up(n, 1)
            use_hot(0)
            use_hot(1)
            shared_up(n, 2)
            for t in range(2, 6):
                use_hot(t)
            for c in range(SC):
                shared_down(n, 0, c)
            use_hot(6)
            use_hot(7)
            for c in range(SC):
                shared_down(n, 1, c)
            pe.wait_ge(expert_counted, 1)
            nc.tensor.matmul(expert_ps, expert_of[:, 1:2], identity, start=True, stop=True).then_inc(expert_turned, 1)
            for t in range(8, T):
                use_hot(t)

            def step(j, k, i, experts):
                static = isinstance(j, int)

                def transpose_rows(j1, k1, i1):
                    pe.wait_ge(gathered[k1], i1 * 16 + 16)
                    wait(pe, c_xTl_made, j1 - 1)
                    for c in range(KC):
                        end = nc.tensor.transpose(gT_ps[:, k1 % 2, c * P:(c + 1) * P],
                                                  rows[:, k1 % R, c * P:(c + 1) * P], identity)
                    end.then_inc(c_xT_done, 1)

                if static and j == 0:
                    transpose_rows(0, 0, 0)
                if not static or j + 1 < ST:
                    transpose_rows(j + 1, (k + 1) % R, i * (U // R) + (k + 1) // R)
                if not static or j < ST:
                    e = experts[k]
                    pe.wait_ge(c_xTl_made, j + 1)
                    wait(pe, c_hidden_made, j - 1)
                    for c in range(KC):
                        at = slice((k % 2) * 2 * P + c * P, (k % 2) * 2 * P + (c + 1) * P)
                        end = split_product(gu_ps[:, k % 2, 0:2 * I], xTh[:, at], xTl[:, at],
                                            W1h[:, bass.ds(e, 1), c, :].rearrange("p e n -> p (e n)"),
                                            W1l[:, bass.ds(e, 1), c, :].rearrange("p e n -> p (e n)"),
                                            c == 0, c == KC - 1)
                    end.then_inc(c_up_done, 1)
                if static and j == 1:
                    pe.wait_ge(low2_made[False], E // 2 - len(BY_POOL2))
                    pe.wait_ge(low2_made[True], len(BY_POOL2))
                if (not static) or 1 <= j <= ST:
                    k1 = (k - 1) % R
                    pe.wait_ge(c_hidden_made, j)
                    wait(pe, c_hTl_made, j - 2)
                    for c in range(IC):
                        end = nc.tensor.transpose(hT_ps[0:IR, k1 % 2, c * P:(c + 1) * P],
                                                  hidden[:, k1 % 2, c * IR:(c + 1) * IR], identity)
                    end.then_inc(c_hT_done, 1)
                if (not static) or 2 <= j <= ST + 1:
                    k2 = (k - 2) % R
                    e = experts[k - 2]
                    pe.wait_ge(c_hTl_made, j - 1)
                    wait(pe, c_y_made, j - 3)
                    for c in range(IC):
                        end = split_product(y_ps[:, k2 % 2, 0:D], hTh[:, k2 % 2, c, :], hTl[:, k2 % 2, c, :],
                                            W2h[:, bass.ds(e, 1), c * D:(c + 1) * D].rearrange("p e n -> p (e n)"),
                                            W2l[:, bass.ds(e, 1), c * D:(c + 1) * D].rearrange("p e n -> p (e n)"),
                                            c == 0, c == IC - 1)
                    end.then_inc(c_down_done, 1)

            pe.wait_ge(expert_made, 1)
            pe.wait_ge(ids_made, 1)
            pe.wait_ge(s_out_made, 2 * NGRP)
            slot_tiles(pe, step, lambda i: turn_experts(pe, i, 0 if isinstance(i, int) and i == 0 else R))

        @block.scalar
        def _(act):
            def copy_xnT(g):
                act.wait_ge(xnT_done, g + 1)
                nc.scalar.copy(xnT[:, :, :, :].rearrange("p t c n -> p (t c n)"),
                               bank[:, 0:2, :].rearrange("p b n -> p (b n)")).then_inc(xnT_made, 1)

            def norm_x(g):
                act.wait_ge(shift_made, g)
                for t in range(G):
                    end = nc.scalar.activation(xn[:, t, :], x_tile(g, t), ACT.Identity, bias=shift[:, t:t + 1],
                                               scale=newton[:, 0, 7, t:t + 1])
                end.then_inc(xn_made, 1)

            def norm_x2(g):
                act.wait_ge(shift2_made, g + 1)
                wait(act, rows_stored, g * 16)
                for t in (2, 3):
                    end = nc.scalar.activation(rows[:, t, 0:D], x_tile(g, t), ACT.Identity, bias=shift2[:, t:t + 1],
                                               scale=newton[:, 1, 7, t:t + 1])
                end.then_inc(x2n_made[1], 1)

            def exp_scores(g):
                act.wait_ge(max_made, g + 1)
                for t in range(G):
                    end = nc.scalar.activation(probs[:, t, :], score_ps[:, t, :], ACT.Exp, bias=small[:, 1, t:t + 1],
                                               scale=D ** -0.5, accum_out=small[:, 2, t:t + 1])
                end.then_inc(exp_made, 1)

            def copy_probsT(g):
                act.wait_ge(probsT_done, g + 1)
                nc.scalar.copy(probsT[:, :, :].rearrange("p t n -> p (t n)"), bank[:, 2, :]).then_inc(probsT_made, 1)

            def high_x2n(g, h):
                act.wait_ge(x2T_done, 2 * g + h + 1)
                nc.scalar.copy(xTh[:, :].rearrange("p (c t n) -> p t c n", c=KC, t=G)[:, 2 * h:2 * h + 2, :, :],
                               x2T_ps[h]).then_inc(xTh_made, 1)

            def exp_logits(g):
                act.wait_ge(logits_shifted, g + 1)
                nc.scalar.activation(router[:, 0, :, :], router[:, 1, :, :], ACT.Exp).then_inc(route_exp, 1)

            def shared_tanh(g, c):
                act.wait_ge(s_up_done, 3 * g + c + 1)
                if c == 0:
                    wait(act, s_last_low_made, g)
                else:
                    wait(act, s_low_made, 2 * g + c - 1)
                r = srows(c)
                nc.scalar.activation(act_s[0:r, c % 2, :], gate_ps[c % 2][0:r, :], ACT.Tanh, scale=0.5
                                     ).then_inc(s_tanh_made, 1)

            def shared_high(g, c):
                act.wait_ge(s_act_made, 3 * g + c + 1)
                if c == 0:
                    wait(act, s_down_done, 2 * g)
                r = srows(c)
                nc.scalar.copy(hsh[0:r, c, :], act_s[0:r, c % 2, :]).then_inc(s_high_made, 1)

            def shared_out(g, h):
                act.wait_ge(s_down_done, 2 * g + h + 1)
                wait(act, shared_stored[h], g * 16)
                nc.scalar.copy(y[:, 2 * h:2 * h + 2, :], outs_ps[h]).then_inc(s_out_made, 1)

            def high(k, dst, cols, value):
                act.wait_ge(raw_in[k], value)
                nc.scalar.copy(dst, raw[:, k, 0:cols]).then_inc(high_made, 1)

            def high_expert(e, k, value):
                high(k, W1h[:, bass.ds(e, 1), :, :].rearrange("p e c n -> p (e c n)"), W1C, value)

            act.wait_ge(consts_in, 16 * 5)
            nc.scalar.activation(gate_tanh[:, :], gates_in[:, :], ACT.Tanh).then_inc(gates_made, 1)
            nc.scalar.copy(Gh, raw_gate[:, :, :])
            nc.scalar.copy(selector_r[:, :], selector[:, :]).then_inc(gate_parts, 1)
            copy_xnT(0)
            high(0, W1sh[:, 0, :], 2 * SI, 16)
            high(1, W1sh[:, 1, :], 2 * SI, 16)
            exp_scores(0)
            copy_probsT(0)
            high(2, W2sh[:, :, :].rearrange("p c n -> p (c n)"), SC * D, 16)
            norm_x(1)
            copy_xnT(1)
            high_expert(0, 3, 16)

            def scale_hot(t):
                act.wait_ge(hot_made, t + 1)
                if t >= HOT:
                    act.wait_ge(hot_used, t - HOT + 1)
                nc.scalar.activation(hot_tile[:, t % HOT, :, :], hot_tile01[:, t % HOT, :, :], ACT.Copy,
                                     scale=const[:, C_ID1 + t:C_ID1 + t + 1]).then_inc(hot_scaled, 1)

            def body(n, front=True):
                def expert(k):
                    high_expert(n * 4 + 4 + k, (3 + k) % 4, n * 16 + (32 if k == 0 else 48))

                exp_logits(n)
                copy_probsT(n + 1)
                shared_tanh(n, 0)
                shared_high(n, 0)
                expert(0)
                if front:
                    norm_x(n + 2)
                shared_tanh(n, 1)
                expert(1)
                shared_tanh(n, 2)
                if front:
                    copy_xnT(n + 2)
                norm_x2(n + 1)
                high_x2n(n + 1, 0)
                high_x2n(n + 1, 1)
                shared_high(n, 1)
                shared_high(n, 2)
                expert(2)
                if front:
                    exp_scores(n + 2)
                else:
                    expert(3)
                    exp_logits(NGRP - 1)
                    act.wait_ge(x2_stored, 16 * NGRP)
                    high2(act, 0)
                    high2(act, 1)
                shared_out(n, 0)
                if front:
                    expert(3)
                shared_out(n, 1)

            norm_x2(0)
            high_x2n(0, 0)
            high_x2n(0, 1)
            exp_scores(1)
            for k in range(1, 4):
                high_expert(k, (3 + k) % 4, 32)
            groups(act, body)
            n = NGRP - 1

            shared_tanh(n, 0)
            shared_high(n, 0)
            scale_hot(0)
            shared_tanh(n, 1)
            shared_high(n, 1)
            shared_tanh(n, 2)
            scale_hot(2)
            high2(act, 2)
            scale_hot(4)
            shared_high(n, 2)
            high2(act, 3)
            scale_hot(6)
            shared_out(n, 0)
            scale_hot(8)
            shared_out(n, 1)
            scale_hot(10)
            high2(act, 4)
            scale_hot(12)
            act.wait_ge(expert_turned, 1)
            nc.scalar.copy(tile_expert[:, :], expert_ps[:, 0:SW]).then_inc(expert_made, 1)
            scale_hot(14)
            for q in range(5, LATE2):
                high2(act, q)

            def step(j, k, i, experts):
                static = isinstance(j, int)

                def high_rows(j1, k1):
                    act.wait_ge(c_xT_done, j1 + 1)
                    nc.scalar.copy(xTh[:, (k1 % 2) * 2 * P:(k1 % 2 + 1) * 2 * P], gT_ps[:, k1 % 2, 0:2 * P]
                                   ).then_inc(c_xTh_made, 1)

                if static and j == 0:
                    high_rows(0, 0)
                if not static or j + 1 < ST:
                    high_rows(j + 1, k + 1)
                if static and j == 0:
                    for q in range(LATE2, E // 2):
                        high2(act, q)
                if not static or j < ST:
                    act.wait_ge(c_up_done, j + 1)
                    nc.scalar.activation(gated[:, k % 2, :], gu_ps[:, k % 2, 0:I], ACT.Tanh, scale=0.5
                                         ).then_inc(c_tanh_made, 1)
                if (not static) or 1 <= j <= ST:
                    act.wait_ge(c_hT_done, j)
                    nc.scalar.copy(hTh[:, (k - 1) % 2, :, :], hT_ps[0:IR, (k - 1) % 2, 0:IC * P].rearrange(
                        "p (c n) -> p c n", c=IC)).then_inc(c_hTh_made, 1)
                if (not static) or 2 <= j <= ST + 1:
                    k2 = (k - 2) % R
                    act.wait_ge(c_down_done, j - 1)
                    wait(act, scattered[k2], (i * (U // R) + (k - 2) // R) * 16)
                    nc.scalar.copy(y[:, k2, :], y_ps[:, k2 % 2, 0:D]).then_inc(c_y_made, 1)

            act.wait_ge(shared_stored[0], 16 * NGRP)
            act.wait_ge(shared_stored[1], 16 * NGRP)
            slot_tiles(act, step)

        @block.vector
        def _(dve):
            def chained(ins, value):
                ins.then_inc(vector_step, 1)
                dve.wait_ge(vector_step, value)

            def chain_over():
                dve.sem_clear(vector_step)

            def moments_of(k, g):
                for t in range(G):
                    end = nc.vector.bn_stats(stats[:, k, t, :],
                                             x_tile(g, t))
                chained(end, 1)
                for t in range(G):
                    end = nc.vector.bn_aggr(moments[:, k, t, :], stats[:, k, t, :])
                end.then_inc(moments_made[k], 1)
                chain_over()

            def rstd_here(g, k):
                n = newton[:, k, :, :]
                dve.wait_ge(moments_made[k], g + 1)
                chained(nc.vector.tensor_scalar(n[:, 0, :], moments[:, k, :, 1], EPS, None, ALU.add), 1)
                nc.vector.tensor_scalar(n[:, 1, :], n[:, 0, :], -0.5, None, ALU.mult)
                chained(nc.vector.tensor_scalar(n[:, 2, :].bitcast(i32), n[:, 0, :].bitcast(i32), -0.5,
                                                float(0x5f3759df), ALU.mult, ALU.add), 2)
                for q, (src, dst) in enumerate(((2, 5), (5, 6), (6, 7))):
                    chained(nc.vector.tensor_tensor(n[:, 3, :], n[:, src, :], n[:, src, :], ALU.mult), 3 + 3 * q)
                    chained(nc.vector.tensor_tensor(n[:, 4, :], n[:, 3, :], n[:, 1, :], ALU.mult), 4 + 3 * q)
                    end = nc.vector.scalar_tensor_tensor(out=n[:, dst, :], in0=n[:, 4, :], scalar=1.5,
                                                         in1=n[:, src, :], op0=ALU.add, op1=ALU.mult)
                    if dst < 7:
                        chained(end, 5 + 3 * q)
                end.then_inc(rstd_made[k], 1)
                chain_over()

            def norm(g, k, dst, tiles=G):
                dve.wait_ge(rstd_made[k], g + 1)
                for t in range(tiles):
                    end = nc.vector.tensor_scalar(dst[:, t, 0:D],
                                                  x_tile(g, t),
                                                  moments[:, k, t, 0:1], newton[:, k, 7, t:t + 1],
                                                  ALU.subtract, ALU.mult)
                return end

            def norm_x(g):
                norm(g, 0, xn).then_inc(xn_made, 1)

            def score_max(g):
                dve.wait_ge(scored, g + 1)
                chained(nc.vector.tensor_reduce(out=small[:, 0, :], in_=score_ps, axis=AX.X, op=ALU.max), 1)
                nc.vector.tensor_scalar(small[:, 1, :], small[:, 0, :], -(D ** -0.5), None, ALU.mult
                                        ).then_inc(max_made, 1)
                chain_over()

            def attend(g):
                dve.wait_ge(exp_made, g + 1)
                chained(nc.vector.reciprocal(small[:, 3, :], small[:, 2, :]), 1)
                chained(nc.vector.tensor_tensor(small[:, 4, :], small[:, 3, :], valid_gate[:, bass.ds(g * G, G)],
                                                ALU.mult), 2)
                chain_over()
                dve.wait_ge(readout_done, g + 1)
                for t in range(G):
                    xt = x_tile(g, t)
                    end = nc.vector.scalar_tensor_tensor(out=xt, in0=read_ps[:, t, :], scalar=small[:, 4, t:t + 1],
                                                         in1=xt, op0=ALU.mult, op1=ALU.add)
                chained(end, 1)
                chain_over()

            def norm_x2(g):
                dve.wait_ge(rstd_made[1], g + 1)
                nc.vector.scalar_tensor_tensor(out=shift2[:, :], in0=moments[:, 1, :, 0], scalar=-1.0,
                                               in1=newton[:, 1, 7, :], op0=ALU.mult, op1=ALU.mult
                                               ).then_inc(shift2_made, 1)
                wait(dve, rows_stored, g * 16)
                norm(g, 1, rows, 2).then_inc(x2n_made[0], 1)

            def low_x2n(g, h):
                dve.wait_ge(xTh_made, 2 * g + h + 1)
                view = [a.rearrange("p (c t n) -> p t c n", c=KC, t=G)[:, 2 * h:2 * h + 2, :, :]
                        for a in (xTl[:, :], xTh[:, :].bitcast(f32))]
                for t in range(2):
                    end = nc.vector.tensor_tensor(view[0][:, t, :, :], x2T_ps[h][:, t, :, :], view[1][:, t, :, :],
                                                  ALU.subtract)
                end.then_inc(xTl_made, 1)

            def route(g, logit_ps=logit_ps):
                dve.wait_ge(logits_done, g + 1)
                chained(nc.vector.tensor_copy(router[:, 0, :, :], logit_ps[:, :, 1, :]), 1)
                chained(nc.vector.tensor_tensor(router[:, 2, :, :], logit_ps[:, :, 0, :], router[:, 0, :, :], ALU.add), 2)
                chained(nc.vector.tensor_reduce(out=rsmall[:, 0, :], in_=router[:, 2, :, :], axis=AX.X, op=ALU.max), 3)
                nc.vector.tensor_tensor(router[:, 1, :, :], router[:, 2, :, :],
                                        rsmall[:, 0, :].unsqueeze(2).to_broadcast([P, G, E]), ALU.subtract
                                        ).then_inc(logits_shifted, 1)
                dve.wait_ge(route_exp, g + 1)
                chained(nc.vector.tensor_reduce(out=rsmall[:, 1, :], in_=router[:, 0, :, :], axis=AX.X, op=ALU.add), 4)
                chained(nc.vector.reciprocal(rsmall[:, 2, :], rsmall[:, 1, :]), 5)
                chained(nc.vector.tensor_tensor(router[:, 1, :, :], router[:, 0, :, :],
                                                rsmall[:, 2, :].unsqueeze(2).to_broadcast([P, G, E]), ALU.mult), 6)
                for t in range(G):
                    end = nc.vector.max(out=top8[:, t, :], in_=router[:, 1, t, :])
                chained(end, 7)
                chained(nc.vector.memset(top8[:, :, TOPK:8], -1.0), 8)
                for t in range(G):
                    end = nc.vector.match_replace(out=router[:, 2, t, :], in_to_replace=top8[:, t, :],
                                                  in_values=router[:, 1, t, :], imm_value=-1.0)
                chained(end, 9)
                now = chosen[:, bass.ds(g * G, G), :]
                chained(nc.vector.tensor_scalar(now, router[:, 2, :, :], 0.0, None, ALU.is_lt), 10)
                wait(dve, weights_stored, g * 16)
                nc.vector.scalar_tensor_tensor(out=rows[:, :, D:ROW], in0=router[:, 1, :, :], scalar=half_tanh[:, :],
                                               in1=now, op0=ALU.mult, op1=ALU.mult).then_inc(weights_made, 1)
                chain_over()

            def shared_act(g, c):
                r = srows(c)
                a = act_s[0:r, c % 2, :]
                dve.wait_ge(s_tanh_made, 3 * g + c + 1)
                chained(nc.vector.scalar_tensor_tensor(out=a, in0=a, scalar=1.0, in1=gate_ps[c % 2][0:r, :],
                                                       op0=ALU.add, op1=ALU.mult), 1)
                nc.vector.scalar_tensor_tensor(out=a, in0=a, scalar=half_tanh[0:r, :], in1=up_ps[c % 2][0:r, :],
                                               op0=ALU.mult, op1=ALU.mult).then_inc(s_act_made, 1)
                chain_over()

            def one_hots(t):
                if t >= HOT:
                    dve.wait_ge(hot_used, t - HOT + 1)
                for of, number, width in ((hot_slot, slot_no, P), (hot_tile01, tile_no, SW)):
                    end = nc.vector.tensor_tensor(of[:, t % HOT, :, :], iotas[:, 0:width, :],
                                                  number[:, t, 0:TOPK].unsqueeze(1).to_broadcast([P, width, TOPK]),
                                                  ALU.is_equal)
                if t % 2:
                    chained(end, 1)
                    end = nc.vector.tensor_scalar(hot_tile[:, t % HOT, :, :], hot_tile01[:, t % HOT, :, :],
                                                  const[:, C_ID1 + t:C_ID1 + t + 1], None, ALU.mult)
                    chain_over()
                end.then_inc(hot_made, 1)

            def ids(ring, j1, k1, made):
                nc.vector.tensor_copy(ring[:, k1:k1 + 1], slot_ids[:, bass.ds(j1, 1)]).then_inc(made, 1)

            dve.wait_ge(x_arrived, 16)
            moments_of(0, 0)
            rstd_here(0, 0)
            norm_x(0)
            def make_bias(tiles):
                nc.vector.tensor_scalar(bias[:, tiles, :], mask_in[:, tiles, :], 1.0, -MASKED, ALU.subtract, ALU.mult
                                        ).then_inc(bias_made, 1)

            dve.wait_ge(consts_in, 16 * 5)
            make_bias(slice(0, G))
            nc.vector.tensor_reduce(out=any_valid[:, :], in_=mask_in, axis=AX.X, op=ALU.max).then_inc(valid_reduced, 1)
            dve.wait_ge(gate_parts, 1)
            nc.vector.tensor_tensor(Gl, raw_gate[:, :, :], Gh.bitcast(f32), ALU.subtract
                                    ).then_inc(gate_parts, 1)
            dve.wait_ge(x_arrived, 32)
            moments_of(0, 1)
            score_max(0)
            dve.wait_ge(gates_made, 1)
            nc.vector.tensor_scalar(half_tanh[:, :], gate_tanh[:, 1:2], 0.5, None, ALU.mult)
            dve.wait_ge(valid_spread, 1)
            nc.vector.tensor_scalar(valid_gate[:, :], valid_ps, gate_tanh[:, 0:1], None, ALU.mult
                                    ).then_inc(valid_made, 1)
            nc.vector.memset(zero[:, :], 0.0).then_inc(zero_made, 1)
            make_bias(slice(G, T))
            nc.vector.tensor_copy(iotas[:, :, :],
                                  const[:, C_IOTA:C_IOTA + P].unsqueeze(2).to_broadcast([P, P, TOPK]))
            nc.vector.tensor_copy(tri[:, :], const[:, C_TRI:C_TRI + P])
            nc.vector.memset(ones[:, :], 1.0)
            nc.vector.memset(prefix[:, :, :], 0.0)
            nc.vector.memset(zeros16[:, :], 0.0).then_inc(routing_consts, 1)
            attend(0)
            moments_of(1, 0)
            rstd_here(0, 1)
            norm_x2(0)

            def body(n, front=True):
                if front:
                    dve.wait_ge(x_arrived, n * 16 + 48)
                    dve.sem_inc(x_seen, 1)
                    moments_of(0, n + 2)
                route(n)
                shared_act(n, 0)
                attend(n + 1)
                moments_of(1, n + 1)
                rstd_here(n + 1, 1)
                norm_x2(n + 1)
                shared_act(n, 1)
                low_x2n(n + 1, 0)
                shared_act(n, 2)
                low_x2n(n + 1, 1)
                shared_low(dve, nc.vector, n, 2)
                if front:
                    score_max(n + 2)

            low_x2n(0, 0)
            low_x2n(0, 1)
            score_max(1)
            groups(dve, body)
            n = NGRP - 1
            route(n, last_logit_ps)

            dve.wait_ge(ranked, 1)
            over = wide[:, 0, :].rearrange("p (e k) -> p e k", e=E)
            chained(nc.vector.tensor_tensor(over, rank_ps[:, T, :].unsqueeze(2).to_broadcast([P, E, T]),
                                            const[:, C_K128:C_K128 + T].unsqueeze(1).to_broadcast([P, E, T]),
                                            ALU.is_gt), 1)
            chained(nc.vector.tensor_reduce(out=tiles_of[:, :], in_=over, axis=AX.X, op=ALU.add), 2)
            chained(nc.vector.tensor_copy(prefix[:, 0, 8:], tiles_of[:, :]), 3)
            for q in range(4):
                d = 1 << q
                chained(nc.vector.tensor_tensor(prefix[:, (q + 1) % 2, 8:], prefix[:, q % 2, 8:],
                                                prefix[:, q % 2, 8 - d:8 + E - d], ALU.add), 4 + q)
            chained(nc.vector.tensor_tensor(base[:, 0, :], prefix[:, 0, 8:], tiles_of[:, :], ALU.subtract), 8)
            chained(nc.vector.tensor_scalar(base[:, 1, :], base[:, 0, :], float(P), 1.0, ALU.mult, ALU.add), 9)
            w0, w1_ = (wide[:, q, :].rearrange("p (t e) -> p t e", e=E) for q in range(2))
            chained(nc.vector.tensor_tensor(w0, rank_ps[:, 0:T, :],
                                            base[:, 1, :].unsqueeze(1).to_broadcast([P, T, E]), ALU.add), 10)
            chained(nc.vector.tensor_tensor(w1_, w0, chosen[:, :, :], ALU.mult), 11)
            for t in range(T):
                end = nc.vector.max(out=places[:, t, :], in_=w1_[:, t, :])
            chained(end, 12)
            flat = places[:, :, :].rearrange("p t k -> p (t k)")
            chained(nc.vector.tensor_scalar(place_bits[:, 0, :], flat, -1.0, None, ALU.add), 13)
            nc.vector.tensor_single_scalar(place_bits[:, 1, :], place_bits[:, 0, :], 7, op=ALU.arith_shift_right)
            chained(nc.vector.tensor_single_scalar(place_bits[:, 2, :], place_bits[:, 0, :], P - 1,
                                                   op=ALU.bitwise_and), 14)
            nc.vector.tensor_copy(tile_no[:, :, :].rearrange("p t k -> p (t k)"), place_bits[:, 1, :])
            nc.vector.tensor_copy(slot_no[:, :, :].rearrange("p t k -> p (t k)"), place_bits[:, 2, :]
                                  ).then_inc(places_made, 1)
            chain_over()
            dve.wait_ge(places_made, 1)
            dve.wait_ge(low_made, 3 + E)
            shared_act(n, 0)
            one_hots(0)
            one_hots(1)
            chained(nc.vector.tensor_scalar(prefix[:, 1, 8:], prefix[:, 0, 8:], const[:, C_ID1:C_ID1 + 1], None,
                                            ALU.is_lt), 1)
            chained(nc.vector.tensor_reduce(out=expert_of[:, 0:1], in_=prefix[:, 1, 8:], axis=AX.X, op=ALU.add), 2)
            nc.vector.tensor_scalar(expert_of[:, 1:2], expert_of[:, 0:1], float(E - 1), None, ALU.min
                                    ).then_inc(expert_counted, 1)
            chain_over()
            shared_act(n, 1)
            for t in range(2, 6):
                one_hots(t)
            shared_act(n, 2)
            shared_low(dve, nc.vector, n, 2)
            for t in range(6, T):
                one_hots(t)
            dve.wait_ge(hot_used, T)
            chained(nc.vector.tensor_scalar(wide[:, 0, 0:SW], inverse_ps, 0.0, const[:, C_PAD:C_PAD + 1],
                                            ALU.is_equal, ALU.mult), 1)
            nc.vector.scalar_tensor_tensor(out=slot_ids[:, :], in0=inverse_ps, scalar=-1.0, in1=wide[:, 0, 0:SW],
                                           op0=ALU.add, op1=ALU.add).then_inc(ids_made, 1)
            chain_over()
            dve.wait_ge(ids_made, 1)
            for q in range(AHEAD + 1):
                ids(gather_ids, q, q, gather_ids_made)
            for q in range(len(BY_POOL2), LATE2):
                low2(dve, nc.vector, q)
            dve.wait_ge(expert_made, 1)

            def step(j, k, i, experts):
                static = isinstance(j, int)

                def low_rows(j1, k1):
                    dve.wait_ge(c_xTh_made, j1 + 1)
                    at = slice((k1 % 2) * 2 * P, (k1 % 2 + 1) * 2 * P)
                    nc.vector.tensor_tensor(xTl[:, at], gT_ps[:, k1 % 2, 0:2 * P], xTh[:, at].bitcast(f32),
                                            ALU.subtract).then_inc(c_xTl_made, 1)

                if static and j == 0:
                    low_rows(0, 0)
                if not static or j + 1 < ST:
                    low_rows(j + 1, k + 1)
                if static and j == 0:
                    for q in range(LATE2, E // 2):
                        low2(dve, nc.vector, q)
                if not static or j < ST:
                    dve.wait_ge(c_tanh_made, j + 1)
                    e = experts[k]
                    g = gated[:, k % 2, :]
                    nc.vector.scalar_tensor_tensor(out=g, in0=g, scalar=1.0, in1=gu_ps[:, k % 2, 0:I],
                                                   op0=ALU.add, op1=ALU.mult).then_inc(c_gated_made, 1)
                    dve.wait_ge(c_gated_made, j + 1)
                    nc.vector.scalar_tensor_tensor(out=hidden[:, k % 2, :], in0=g, scalar=rows[:, k % R, bass.ds(e + D, 1)],
                                                   in1=gu_ps[:, k % 2, I:2 * I], op0=ALU.mult, op1=ALU.mult
                                                   ).then_inc(c_hidden_made, 1)
                if not static or j + R < ST:
                    ids(gather_ids, j + R, k % R, gather_ids_made)
                if (not static) or 2 <= j <= ST + 1:
                    wait(dve, scattered[(k - 2) % R], (i * (U // R) + (k - 2) // R) * 16)
                if (not static) or 1 <= j <= ST:
                    k1 = (k - 1) % 2
                    dve.wait_ge(c_hTh_made, j)
                    nc.vector.tensor_tensor(hTl[:, k1, :, :], hT_ps[0:IR, k1, 0:IC * P].rearrange("p (c n) -> p c n", c=IC),
                                            hTh[:, k1, :, :].bitcast(f32), ALU.subtract).then_inc(c_hTl_made, 1)
                if (not static) or 2 <= j <= ST + 1:
                    k2 = (k - 2) % R
                    ids(scatter_ids, j - 2, k2, scatter_ids_made)

            slot_tiles(dve, step, lambda i: turn_experts(dve, i, 0))

            for g in range(NGRP):
                dve.wait_ge(parts_in[g], 32)
                a, b = (part[:, g, q, :, :].rearrange("p t d -> p (t d)") for q in range(2))
                nc.vector.tensor_tensor(a, a, b, ALU.add).then_inc(summed, 1)

        @block.gpsimd
        def _(pool):
            def rstd(g):
                n = newton[:, 0, :, :]
                step = [0]

                def chained(ins):
                    step[0] += 1
                    ins.then_inc(pool_step, 1)
                    pool.wait_ge(pool_step, step[0])

                pool.wait_ge(moments_made[0], g + 1)
                chained(nc.gpsimd.tensor_tensor(n[:, 0, :], moments[:, 0, :, 1], eps[:, :], ALU.add))
                nc.gpsimd.tensor_scalar(n[:, 1, :], n[:, 0, :], -0.5, None, ALU.mult)
                chained(nc.gpsimd.tensor_scalar(n[:, 2, :].bitcast(i32), n[:, 0, :].bitcast(i32), -0.5,
                                                float(0x5f3759df), ALU.mult, ALU.add))
                for src, dst in ((2, 5), (5, 6), (6, 7)):
                    chained(nc.gpsimd.tensor_tensor(n[:, 3, :], n[:, src, :], n[:, src, :], ALU.mult))
                    chained(nc.gpsimd.tensor_tensor(n[:, 4, :], n[:, 3, :], n[:, 1, :], ALU.mult))
                    chained(nc.gpsimd.tensor_scalar(n[:, 3, :], n[:, 4, :], 1.5, None, ALU.add))
                    end = nc.gpsimd.tensor_tensor(n[:, dst, :], n[:, 3, :], n[:, src, :], ALU.mult)
                    chained(end)
                chained(nc.gpsimd.tensor_tensor(n[:, 3, :], n[:, 7, :], moments[:, 0, :, 0], ALU.mult))
                nc.gpsimd.tensor_scalar(shift[:, :], n[:, 3, :], -1.0, None, ALU.mult).then_inc(shift_made, 1)
                pool.sem_clear(pool_step)

            def low(dst, k, high, cols, value):
                pool.wait_ge(high_made, value)
                nc.gpsimd.tensor_tensor(dst, raw[:, k, 0:cols], high, ALU.subtract).then_inc(low_made, 1)

            def low_expert(e, k, value):
                low(W1l[:, bass.ds(e, 1), :, :].rearrange("p e c n -> p (e c n)"), k,
                    W1h[:, bass.ds(e, 1), :, :].bitcast(f32).rearrange("p e c n -> p (e c n)"), W1C, value)

            nc.gpsimd.memset(eps[:, :], EPS).then_inc(pool_step, 1)
            pool.wait_ge(pool_step, 1)
            pool.sem_clear(pool_step)
            rstd(1)
            for k in range(2):
                low(W1sl[:, k, :], k, W1sh[:, k, :].bitcast(f32), 2 * SI, k + 1)
            low(W2sl[:, :, :].rearrange("p c n -> p (c n)"), 2, W2sh[:, :, :].bitcast(f32).rearrange("p c n -> p (c n)"),
                SC * D, 3)
            for k in range(4):
                low_expert(k, (3 + k) % 4, 4 + k)

            def body(n, front=True):
                def expert(k):
                    low_expert(n * 4 + 4 + k, (3 + k) % 4, n * 4 + 8 + k)

                if front:
                    rstd(n + 2)
                shared_low(pool, nc.gpsimd, n, 0)
                expert(0)
                shared_low(pool, nc.gpsimd, n, 1)
                expert(1)
                expert(2)
                expert(3)

            groups(pool, body)

            for q in BY_POOL2:
                low2(pool, nc.gpsimd, q)
                if q == 1:
                    for c in range(2):
                        shared_low(pool, nc.gpsimd, NGRP - 1, c)

            def no_wait_in_dma():
                pool.sem_inc(dma_allowed, 1)

            def gather(j, k):
                pool.wait_ge(gather_ids_made, j + 1)
                no_wait_in_dma()
                nc.gpsimd.indirect_dma_start(
                    out=rows[:, k, :], out_offset=None, in_=rows_dram,
                    in_offset=bass.IndirectOffsetOnAxis(ap=gather_ids[:, k:k + 1], axis=0),
                    bounds_check=N + P - 1).then_inc(gathered[k], 16)

            def step(j, k, i, experts):
                static = isinstance(j, int)
                if static and j == 0:
                    for q in range(AHEAD):
                        gather(q, q)
                if not static or j + AHEAD < ST:
                    wait(pool, c_hidden_made, j)
                    gather(j + AHEAD, (k + AHEAD) % R)
                if not static or j >= 3:
                    k3 = (k - 3) % R
                    wait(pool, scattered[(k - 5) % R], (i * (U // R) + (k - 5) // R + 1) * 16)
                    pool.wait_ge(scatter_ids_made, j - 2)
                    pool.wait_ge(c_y_made, j - 2)
                    no_wait_in_dma()
                    nc.gpsimd.indirect_dma_start(
                        out=sums[k3 % 2], out_offset=bass.IndirectOffsetOnAxis(ap=scatter_ids[:, k3:k3 + 1], axis=0),
                        in_=y[:, k3, :], in_offset=None, bounds_check=N + P - 1,
                        compute_op=ALU.add).then_inc(scattered[k3], 16)

            pool.wait_ge(ids_made, 1)
            pool.wait_ge(pads_stored, 16 * 3)
            pool.wait_ge(rows_stored, 16 * NGRP)
            pool.wait_ge(weights_stored, 16 * NGRP)
            pool.wait_ge(x2_stored, 16 * NGRP)
            for h in range(2):
                pool.wait_ge(shared_stored[h], 16 * NGRP)
            slot_tiles(pool, step)


def kernel(x, ctx_2048, mask_BxS2_bk0, g_xattn, g_ffn, L0_ffn_gate_w, L0_ffn_w1, L0_ffn_w2,
           L0_ffn_shared_w1, L0_ffn_shared_w2):
    import numpy as np
    import concourse.bacc as bacc
    from concourse.bass_utils import run_bass_kernel_spmd

    c, f = np.ascontiguousarray, np.float32
    x, ctx = np.asarray(x).reshape(N, D), np.asarray(ctx_2048).reshape(N, D)
    ctx_t = c(ctx.reshape(T, P, KC, P).transpose(3, 0, 2, 1))
    mask = np.zeros((BT, T, P), np.uint8)
    bits = np.asarray(mask_BxS2_bk0).view(np.uint8).reshape(T, BT, M)
    for b in range(BT):
        mask[b, :, b * M:(b + 1) * M] = bits[:, b, :]
    mask = mask.view(np.int32)
    gates = c(np.broadcast_to(np.concatenate([np.asarray(g_xattn), np.asarray(g_ffn)])[None, :], (P, 2)))
    gate_w = c(np.asarray(L0_ffn_gate_w).T.reshape(KC, P, E).transpose(1, 0, 2))
    w1 = c(np.asarray(L0_ffn_w1).reshape(E, 2 * I, KC, P).transpose(0, 3, 2, 1).reshape(E, P, W1C))
    w1s = c(np.asarray(L0_ffn_shared_w1).reshape(2 * SI, KC, P).transpose(2, 1, 0))
    w2 = c(np.asarray(L0_ffn_w2).reshape(E, D, IC, IR).transpose(3, 0, 2, 1).reshape(IR, E, IC * D))
    w2s = np.concatenate([np.asarray(L0_ffn_shared_w2).T, np.zeros((SC * P - SI, D), f)])
    w2s = c(w2s.reshape(SC, P, D).transpose(1, 0, 2).reshape(P, SC * D))
    n = np.arange(P)
    consts = np.zeros((P, C_END), f)
    consts[:, C_IDENT:C_IDENT + P] = np.eye(P)
    consts[:, C_IOTA:C_IOTA + P] = n[None, :]
    consts[:, C_TRI:C_TRI + P] = n[:, None] < n[None, :]
    consts[:, C_K128:C_K128 + T] = P * np.arange(T)[None, :]
    consts[:, C_ID1:C_ID1 + T] = P * np.arange(T)[None, :] + n[:, None] + 1
    consts[:, C_PAD] = N + 1 + n
    sel = c(np.repeat(np.eye(BT, dtype=f), S, axis=1))

    arrays = {"x": x, "ctx_n": ctx, "ctx_t": ctx_t, "mask": mask, "gates": gates, "gate_w": gate_w,
              "w1": w1, "w1s": w1s, "w2": w2, "w2s": w2s, "consts": consts, "sel": sel}
    nc = bacc.Bacc("TRN2", target_bir_lowering=False, num_devices=1)
    args = {k: nc.dram_tensor("in_" + k, a.shape, mybir.dt.from_np(a.dtype), kind="ExternalInput").ap()
            for k, a in arrays.items()}
    out = nc.dram_tensor("out", (N, D), mybir.dt.float32, kind="ExternalOutput").ap()
    sparse_block(nc, out=out, **args)
    r = run_bass_kernel_spmd(nc, [{"in_" + k: c(a) for k, a in arrays.items()}], core_ids=[0])
    return r.results[0]["out"].reshape(B, S, D)
```
